# Optimizing a Trainium2 kernel written in Bass

```python
import numpy as np
import jax
import jax.numpy as jnp

def _softmax(x, axis=-1):
    return jax.nn.softmax(x, axis=axis)

def _gelu(x):
    return jax.nn.gelu(x, approximate=True)

def _silu(x):
    return jax.nn.silu(x)

def _sigmoid(x):
    return jax.nn.sigmoid(x)

def _layernorm(x, axis=-1, eps=1e-05):
    m = jnp.mean(x, axis=axis, keepdims=True)
    v = jnp.var(x, axis=axis, keepdims=True)
    return (x - m) / jnp.sqrt(v + eps)

def _scatter_add(tgt, idx, src, axis=0):
    return tgt.at[idx].add(src)

def _segment_sum(src, seg, n):
    return jax.ops.segment_sum(src, seg, n)
kernel_name = 'mk_lm_tower_d1_tok_ids512_r4_e4caa2'

def setup_inputs(seed: int=0):
    np.random.seed(seed)
    _w = jnp.asarray

    def _rec_inputs():
        import jax
        import jax.numpy as jnp
        _rk = jax.random.key(seed)
        x = jax.random.randint(jax.random.fold_in(_rk, 1), (8, 256), 0, 10000, jnp.int32)
        return x
    x = _rec_inputs()

    def _L0_tok_setup():
        import jax, jax.numpy as jnp
        import numpy as np
        B, S, H = (64, 512, 128)
        VOCAB = 10000

        def _syntax_info(token_ids):
            t = token_ids
            opens = (t == 40) | (t == 123) | (t == 91)
            closes = (t == 41) | (t == 125) | (t == 93)
            delta = opens.astype(jnp.int32) - closes.astype(jnp.int32)
            s = jnp.cumsum(delta, axis=1)
            run_min = jax.lax.cummin(s, axis=1)
            nesting = jnp.clip(s - jnp.minimum(run_min, 0), 0, 15)
            segments = jnp.cumsum((t > 39990).astype(jnp.int32), axis=1) % 8
            return (nesting, segments)
        key = jax.random.key(seed)
        k1, k2, k3, k4, k5 = jax.random.split(key, 5)
        token_ids = jax.random.randint(k1, (B, S), 0, VOCAB, dtype=jnp.int64) if jax.config.jax_enable_x64 else jax.random.randint(k1, (B, S), 0, VOCAB, dtype=jnp.int32)
        std = 0.02
        pos_table = jax.random.normal(k2, (S, H), dtype=jnp.float32) * std
        nest_table = jax.random.normal(k3, (16, H), dtype=jnp.float32) * std
        seg_table = jax.random.normal(k4, (8, H), dtype=jnp.float32) * std
        W = jax.random.normal(k5, (3 * H, H), dtype=jnp.float32) * (1.0 / np.sqrt(3 * H))
        return {'token_ids': token_ids, 'pos_table': pos_table, 'nest_table': nest_table, 'seg_table': seg_table, 'W': W}
    _L0_tok_all = _L0_tok_setup()
    _L0_tok_in = {k: v for k, v in _L0_tok_all.items() if k in ('pos_table', 'nest_table', 'seg_table', 'W')}
    del _L0_tok_all

    def _L0_attn_setup():
        import jax, jax.numpy as jnp
        import numpy as np
        HEAD_NUMS = 8
        LN_EPS = 1e-05

        def _layernorm(x, g, b):
            m = jnp.mean(x, axis=-1, keepdims=True)
            v = jnp.var(x, axis=-1, keepdims=True)
            return (x - m) * jax.lax.rsqrt(v + LN_EPS) * g + b
        key = jax.random.key(seed)
        ks = jax.random.split(key, 6)
        B, S, D = (4, 512, 128)
        x = jax.random.normal(ks[0], (B, S, D), dtype=jnp.float32)
        W1 = jax.random.normal(ks[1], (4 * D, D), dtype=jnp.float32) * 0.02
        b1 = jnp.zeros((4 * D,), dtype=jnp.float32)
        ln_g = jnp.ones((D,), dtype=jnp.float32)
        ln_b = jnp.zeros((D,), dtype=jnp.float32)
        W2 = jax.random.normal(ks[2], (D, D), dtype=jnp.float32) * 0.02
        b2 = jnp.zeros((D,), dtype=jnp.float32)
        return {'x': x, 'W1': W1, 'b1': b1, 'ln_g': ln_g, 'ln_b': ln_b, 'W2': W2, 'b2': b2}
    _L0_attn_all = _L0_attn_setup()
    _L0_attn_in = {k: v for k, v in _L0_attn_all.items() if k in ('W1', 'b1', 'ln_g', 'ln_b', 'W2', 'b2')}
    del _L0_attn_all

    def _L0_ffn_setup():
        import jax, jax.numpy as jnp
        import numpy as np
        NUM_EXPERTS = 8
        TOP_K = 2
        key = jax.random.key(seed)
        k0, k1, k2, k3, k4 = jax.random.split(key, 5)
        sl, bs, hs, ffn = (512, 2, 128, 512)
        T = sl * bs
        x = jax.random.normal(k0, (sl, bs, hs), jnp.float32)
        expert_weights = jax.random.uniform(k1, (T, TOP_K), jnp.float32)
        expert_indices = jax.random.randint(k2, (T, TOP_K), 0, NUM_EXPERTS)
        w1 = jax.random.normal(k3, (NUM_EXPERTS, hs, ffn), jnp.float32) * hs ** (-0.5)
        w2 = jax.random.normal(k4, (NUM_EXPERTS, ffn, hs), jnp.float32) * ffn ** (-0.5)
        return dict(x=x, expert_weights=expert_weights, expert_indices=expert_indices, w1=w1, w2=w2)
    _L0_ffn_all = _L0_ffn_setup()
    _L0_ffn_in = {k: v for k, v in _L0_ffn_all.items() if k in ('expert_weights', 'expert_indices', 'w1', 'w2')}
    del _L0_ffn_all
    return {'x': x, 'L0_tok_pos_table': _L0_tok_in['pos_table'], 'L0_tok_nest_table': _L0_tok_in['nest_table'], 'L0_tok_seg_table': _L0_tok_in['seg_table'], 'L0_tok_W': _L0_tok_in['W'], 'L0_attn_W1': _L0_attn_in['W1'], 'L0_attn_b1': _L0_attn_in['b1'], 'L0_attn_ln_g': _L0_attn_in['ln_g'], 'L0_attn_ln_b': _L0_attn_in['ln_b'], 'L0_attn_W2': _L0_attn_in['W2'], 'L0_attn_b2': _L0_attn_in['b2'], 'L0_ffn_expert_weights': _L0_ffn_in['expert_weights'], 'L0_ffn_expert_indices': _L0_ffn_in['expert_indices'], 'L0_ffn_w1': _L0_ffn_in['w1'], 'L0_ffn_w2': _L0_ffn_in['w2']}

def reference(x, L0_tok_pos_table, L0_tok_nest_table, L0_tok_seg_table, L0_tok_W, L0_attn_W1, L0_attn_b1, L0_attn_ln_g, L0_attn_ln_b, L0_attn_W2, L0_attn_b2, L0_ffn_expert_weights, L0_ffn_expert_indices, L0_ffn_w1, L0_ffn_w2):
    import jax
    import jax.numpy as jnp

    def _L0_tok_ref(token_ids, pos_table, nest_table, seg_table, W):
        import jax, jax.numpy as jnp
        import numpy as np
        B, S, H = (64, 512, 128)
        VOCAB = 10000

        def _syntax_info(token_ids):
            t = token_ids
            opens = (t == 40) | (t == 123) | (t == 91)
            closes = (t == 41) | (t == 125) | (t == 93)
            delta = opens.astype(jnp.int32) - closes.astype(jnp.int32)
            s = jnp.cumsum(delta, axis=1)
            run_min = jax.lax.cummin(s, axis=1)
            nesting = jnp.clip(s - jnp.minimum(run_min, 0), 0, 15)
            segments = jnp.cumsum((t > 39990).astype(jnp.int32), axis=1) % 8
            return (nesting, segments)
        b, s = token_ids.shape
        positions = jnp.arange(s)
        pos_emb = jnp.broadcast_to(pos_table[positions][None], (b, s, pos_table.shape[-1]))
        nesting, segments = _syntax_info(token_ids)
        nest_emb = nest_table[nesting]
        seg_emb = seg_table[segments]
        combined = jnp.concatenate([pos_emb, nest_emb, seg_emb], axis=-1)
        return jnp.einsum('bsk,kh->bsh', combined, W)

    def _L0_attn_ref(x, W1, b1, ln_g, ln_b, W2, b2):
        import jax, jax.numpy as jnp
        import numpy as np
        HEAD_NUMS = 8
        LN_EPS = 1e-05

        def _layernorm(x, g, b):
            m = jnp.mean(x, axis=-1, keepdims=True)
            v = jnp.var(x, axis=-1, keepdims=True)
            return (x - m) * jax.lax.rsqrt(v + LN_EPS) * g + b
        B, S, D = x.shape
        H = HEAD_NUMS
        hd = D // H
        h = jax.nn.silu(x @ W1.T + b1)
        h = h.reshape(B, S, 4, H, hd)
        gate = jnp.transpose(h[:, :, 0], (0, 2, 1, 3))
        q = jnp.transpose(h[:, :, 1], (0, 2, 1, 3))
        k = jnp.transpose(h[:, :, 2], (0, 2, 1, 3))
        v = jnp.transpose(h[:, :, 3], (0, 2, 1, 3))
        scale = 1.0 / np.sqrt(hd).astype(np.float32)
        scores = jnp.einsum('bhsd,bhtd->bhst', q, k) * scale
        causal = jnp.tril(jnp.ones((S, S), dtype=bool))
        a = jnp.where(causal, jax.nn.silu(scores), 0.0)
        o = jnp.einsum('bhst,bhtd->bhsd', a, v)
        o = jnp.transpose(o, (0, 2, 1, 3)).reshape(B, S, D)
        normed = _layernorm(o, ln_g, ln_b)
        gate_f = jnp.transpose(gate, (0, 2, 1, 3)).reshape(B, S, D)
        return normed * gate_f @ W2.T + b2

    def _L0_ffn_ref(x, expert_weights, expert_indices, w1, w2):
        import jax, jax.numpy as jnp
        import numpy as np
        NUM_EXPERTS = 8
        TOP_K = 2
        'Dropless MoE: sort assignments by expert, gather tokens, grouped MLP,\n            scatter-combine with top-k router weights (megablocks gather/scatter semantics).'
        in_shape = x.shape
        hs = in_shape[-1]
        x_flat = x.reshape(-1, hs)
        T = x_flat.shape[0]
        flat_ids = expert_indices.reshape(-1)
        order = jnp.argsort(flat_ids)
        bin_ids = flat_ids[order]
        token_ids = order // TOP_K
        xg = x_flat[token_ids]
        y = jnp.zeros_like(xg)
        for e in range(NUM_EXPERTS):
            h = jax.nn.gelu(xg @ w1[e], approximate=False)
            y = jnp.where((bin_ids == e)[:, None], h @ w2[e], y)
        w = expert_weights.reshape(-1)[order][:, None]
        out = jnp.zeros((T, hs), x.dtype).at[token_ids].add(w * y)
        return out.reshape(in_shape)
    h = _L0_tok_ref(x, L0_tok_pos_table, L0_tok_nest_table, L0_tok_seg_table, L0_tok_W)
    h = h + _L0_attn_ref(_layernorm(h, axis=-1), L0_attn_W1, L0_attn_b1, L0_attn_ln_g, L0_attn_ln_b, L0_attn_W2, L0_attn_b2)
    h = h + _L0_ffn_ref(_layernorm(h, axis=-1), L0_ffn_expert_weights, L0_ffn_expert_indices, L0_ffn_w1, L0_ffn_w2)
    return h

_drawn_inputs = setup_inputs


def setup_inputs(seed=0):
    import zlib

    import numpy as np

    out = dict(_drawn_inputs(seed))
    spreads = {'L0_attn_b1': (0.0, 0.1),
     'L0_attn_ln_g': (1.0, 0.2),
     'L0_attn_ln_b': (0.0, 0.297),
     'L0_attn_b2': (0.0, 0.1)}
    factors = {}
    for name, (base, spread) in spreads.items():
        noise = np.random.default_rng([zlib.crc32(name.encode()), seed]).standard_normal(out[name].shape)
        drawn = base * np.exp(spread * noise) if base else spread * noise
        out[name] = jnp.asarray(drawn.astype(out[name].dtype))
    for name, factor in factors.items():
        out[name] = (out[name] * factor).astype(out[name].dtype)
    return out
```

```python
import concourse.bass as bass
from concourse import mybir
from contextlib import ExitStack

F32, BF16, I32 = mybir.dt.float32, mybir.dt.bfloat16, mybir.dt.int32
ALU = mybir.AluOpType
ACT = mybir.ActivationFunctionType

P = 128
B, S, D = 8, 256, 128
CH = S // P
NC = B * CH
H, HD = 8, 16
NEST, SEG = 16, 8
PIECES = ((0, 0), (0, 1), (1, 0), (0, 2), (1, 1), (2, 0))
KS = HD * len(PIECES)
SC = S + P
HALVES = ((0, 2, 4, 6), (1, 3, 5, 7))
E, FF = 8, 512
FC = FF // P
TM = 1024
MC = TM // P
TT = 512
EPS = 1e-5
R = 4


def build(nc, x, pos_table, nest_table, seg_table, tok_W, W1, b1, ln_g, ln_b, W2, b2, route_w, route_e, w1, w2, out):
    ctx = ExitStack()
    with ctx:
        def sb(name, shape, dt=F32):
            return ctx.enter_context(nc.sbuf_tensor(name, shape, dt))

        def pb(name):
            return ctx.enter_context(nc.psum_tensor(name, [P, 512], F32))

        def sem(name):
            return ctx.enter_context(nc.semaphore(name))

        ident = sb("ident", [P, P])
        ids = sb("ids", [B, S], I32)
        nest_sb = sb("nest_sb", [NEST, D])
        seg_sb = sb("seg_sb", [SEG, D])
        tokW_sb = sb("tokW_sb", [P, 3, D])
        pos_sb = sb("pos_sb", [P, CH, D])
        W1_sb = sb("W1_sb", [P, 4, D])
        W2_sb = sb("W2_sb", [P, D])
        rows6 = sb("rows6", [6, P])
        cols6 = sb("cols6", [P, 6])
        b1_cols, g_col, b_col = cols6[:, 0:4], cols6[:, 4:5], cols6[:, 5:6]
        W1T = sb("W1T", [P, 4, P])
        W2T = sb("W2T", [P, D])
        posT = sb("posT", [P, CH, P])
        tabT = sb("tabT", [P, 2, P])
        PW = sb("PW", [P, CH, D])
        raw = sb("raw", [P, 3, D])
        rest = sb("rest", [P, 3, D])
        piece2 = sb("piece2", [P, 3, D], BF16)
        rhs_pieces = sb("rhs_pieces", [P, 3, D], BF16)
        ones_bf = sb("ones_bf", [P, P], BF16)
        cmpf = sb("cmpf", [B, 7, S])
        delta = sb("delta", [B, S])
        depth = sb("depth", [B, S])
        lowest = sb("lowest", [B, S])
        nestf = sb("nestf", [B, S])
        segf = sb("segf", [B, S])
        segi = sb("segi", [B, S], I32)
        segi8 = sb("segi8", [B, S], I32)
        zeroB = sb("zeroB", [B, S])
        code = sb("code", [B, 2, S], BF16)
        sel = sb("sel", [B, 2, B, P], BF16)
        rowi = sb("rowi", [P, 1], I32)
        row32 = sb("row32", [P, 1], I32)
        rowf = sb("rowf", [P, 1])
        rowge = sb("rowge", [P, 1])
        rowcode = sb("rowcode", [P, 1])
        onehot = sb("onehot", [P, B, S], BF16)
        h_all = sb("h_all", [P, NC, D])
        bst = sb("bst", [P, 2, CH, 6])
        mv1 = sb("mv1", [P, 2, CH, 2])
        ve1 = sb("ve1", [P, 2, CH])
        rs1 = sb("rs1", [P, 2, CH])
        mhalf = sb("mhalf", [P, MC])
        xn = sb("xn", [P, 2, CH, D])
        xT = sb("xT", [P, 2, S])
        qk = sb("qk", [P, 2, 2, S])
        qkp = [sb(f"qkp{i}", [P, 2, 2, S], BF16) for i in range(3)]
        qkr = sb("qkr", [P, 2, 2, S])
        stacks = sb("stacks", [KS, R, 2, H, S], BF16)
        bounce = nc.dram_tensor("bounce", (2, 3, P, 2, S), BF16, kind="Internal").ap()
        gate = sb("gate", [P, R, S])
        vpad = sb("vpad", [P, R, CH, H, 32])
        probs = sb("probs", [P, 4, 2, SC])
        oT = sb("oT", [P, S])
        bst2 = sb("bst2", [P, CH, 6])
        mv2 = sb("mv2", [P, CH, 2])
        ve2 = sb("ve2", [P, CH])
        rs2 = sb("rs2", [P, CH])
        xo = sb("xo", [P, CH, D])
        xa = sb("xa", [P, S])
        z = sb("z", [P, S])
        w1_sb = sb("w1_sb", [P, E, FF])
        w2_sb = sb("w2_sb", [P, E, FC, D])
        re_i = sb("re_i", [P, MC, 2], I32)
        re_f = sb("re_f", [P, MC, 2])
        rw = sb("rw", [P, MC, 2])
        coef = sb("coef", [P, 2, E, MC])
        coefs = sb("coefs", [P, E, MC])
        bst3 = sb("bst3", [P, MC, 6])
        mv3 = sb("mv3", [P, MC, 2])
        ve3 = sb("ve3", [P, MC])
        rs3 = sb("rs3", [P, MC])
        xm = sb("xm", [P, MC, D])
        xmT = sb("xmT", [P, TM])
        hid = sb("hid", [P, 2, FC, TT])

        bank = [pb(f"bank{i}") for i in range(8)]
        SCORE, PROJ, OUTC, OTB, XB = (0, 1, 2, 3), bank[4], bank[5], bank[6], bank[7]

        names = """ids_in small_in cols_in attnw_in bias_in pos_in rts_in w1_in w2_in ident0 ident_ready sel0 sel_ready
        consts rows idx_ready cmp del dep low nst sgi sgf code_ready tab0 tr_ps tabs_ready w1t_ps w1t_ready pw_ps pw_ready nw_ps raw0 raw_ready
        pc1 pc2 pc3 pc4 pieces_ready code_ps onehot_ready embed_ps h_ready st1 mv1_s ve1_s rs1_s xn_ready xt_ps xt_ready
        qk_ps qk_ready gv_ps g_ready v_ready p1_s r1_s p2_s p3_s scores_ps probs_ready masked av_done ot_ready o_ps st2 mv2_s ve2_s rs2_s
        xo_ready xot_ps xa_ready z_ready y_ps h2_ready stored vz cf0 cf1 coef_ready st3 mv3_s ve3_s rs3_s xm_ready xmt_ps xmt_ready
        hid_ps hid_ready ye_ps acc_ready"""
        s = {n: sem(n) for n in names.split()}
        stk = [sem(f"stacks_in{i}") for i in range(R)]
        bounced = [sem(f"bounced{i}") for i in range(3)]
        NDMA = 2 * len(PIECES)
        block = ctx.enter_context(nc.Block())

        @block.sync
        def _(sp):
            sp.dma_start(ids[:, :], x).then_inc(s["ids_in"], 16)
            sp.dma_start(nest_sb[:, :], nest_table).then_inc(s["small_in"], 16)
            sp.dma_start(seg_sb[:, :], seg_table).then_inc(s["small_in"], 16)
            sp.dma_start(tokW_sb[:, :, :], tok_W.rearrange("(k p) n -> p k n", p=P)).then_inc(s["small_in"], 16)
            sp.dma_start(pos_sb[:, :, :], pos_table[0:S, :].rearrange("(c p) n -> p c n", p=P)).then_inc(s["pos_in"], 16)
            sp.dma_start(W1_sb[:, :, :], W1.rearrange("(k p) n -> p k n", p=P)).then_inc(s["attnw_in"], 16)
            sp.dma_start(W2_sb[:, :], W2).then_inc(s["attnw_in"], 16)
            sp.dma_start(rows6[0:4, :], b1.rearrange("(k p) -> k p", p=P)).then_inc(s["cols_in"], 16)
            sp.dma_start(rows6[4:5, :], ln_g.rearrange("(a p) -> a p", a=1)).then_inc(s["cols_in"], 16)
            sp.dma_start(rows6[5:6, :], ln_b.rearrange("(a p) -> a p", a=1)).then_inc(s["cols_in"], 16)
            sp.wait_ge(s["raw0"], 1)
            for r in range(3):
                sp.dma_start(raw[32 * r:32 * r + 1, 1, :], b1[3 * P:4 * P].rearrange("(a n) -> a n", a=1)).then_inc(s["bias_in"], 16)
                sp.dma_start(raw[32 * r:32 * r + 1, 2, :], b2.rearrange("(a n) -> a n", a=1)).then_inc(s["bias_in"], 16)
            sp.dma_start(re_i[:, :, :], route_e.rearrange("(c p) k -> p c k", p=P)).then_inc(s["rts_in"], 16)
            sp.dma_start(rw[:, :, :], route_w.rearrange("(c p) k -> p c k", p=P)).then_inc(s["rts_in"], 16)

            def stack(b):
                q = b % 2
                if b >= 2:
                    sp.wait_ge(stk[(b - 2) % R], 16 * NDMA * ((b - 2) // R + 1))
                for piece in range(3):
                    sp.wait_ge(s[("p1_s", "p2_s", "p3_s")[piece]], b + 1)
                    sp.dma_start(bounce[q, piece], qkp[piece][:, q, :, :]).then_inc(bounced[piece], 16)
                if b >= R:
                    sp.wait_ge(s["scores_ps"], 4 * (b - R + 1))
                for piece in range(3):
                    sp.wait_ge(bounced[piece], 16 * (b + 1))
                    for slot, pair in enumerate(PIECES):
                        for side in range(2):
                            if pair[side] == piece:
                                sp.dma_start(stacks[HD * slot:HD * (slot + 1), b % R, side, :, :],
                                             bounce[q, piece, :, side, :].rearrange("(h r) s -> r h s", r=HD)).then_inc(stk[b % R], 16)

            def store(b):
                sp.wait_ge(s["h2_ready"], b + 1)
                sp.dma_start(out[b].rearrange("(c p) d -> p c d", p=P), h_all[:, CH * b:CH * b + CH, :]).then_inc(s["stored"], 16)

            stack(0)
            sp.dma_start(w1_sb[:, :, :], w1.rearrange("e p f -> p e f")).then_inc(s["w1_in"], 16)
            sp.dma_start(w2_sb[:, :, :, :].rearrange("p e c d -> p (e c) d"), w2.rearrange("e (c p) d -> p (e c) d", p=P)).then_inc(s["w2_in"], 16)
            for b in range(1, B):
                stack(b)
            for b in range(TM // S, B):
                store(b)
            for c in range(MC):
                sp.wait_ge(s["acc_ready"], (E - 1) * MC + c + 1)
                sp.dma_start(out[c // CH, P * (c % CH):P * (c % CH) + P, :], h_all[:, c, :]).then_inc(s["stored"], 16)
            sp.wait_ge(s["stored"], 16 * (B - TM // S + MC))

        @block.gpsimd
        def _(pool):
            g = nc.gpsimd
            g.memset(ident[:, :], 0.0).then_inc(s["ident0"], 1)
            g.memset(sel[:, :, :, :], 0.0).then_inc(s["sel0"], 1)
            pool.wait_ge(s["ident0"], 1)
            g.affine_select(out=ident[:, :], in_=ident[:, :], compare_op=ALU.not_equal, fill=1.0, base=0,
                            pattern=[[-1, P]], channel_multiplier=1).then_inc(s["ident_ready"], 1)
            g.iota(rowi[:, :], pattern=[[0, 1]], base=0, channel_multiplier=1).then_inc(s["rows"], 1)
            pool.wait_ge(s["sel0"], 1)
            v = sel[:, :, :, :].rearrange("k t b (q r) -> k t b q r", r=32)
            for t in range(2):
                for r in range(3):
                    g.memset(v[:, t, :, r, 16 * t:16 * t + (NEST, SEG)[t]], 1.0).then_inc(s["sel0"], 1)
            pool.wait_ge(s["sel0"], 7)
            for t in range(2):
                g.affine_select(out=sel[:, t, :, :], in_=sel[:, t, :, :], compare_op=ALU.is_equal, fill=0.0, base=0,
                                pattern=[[1, B], [0, P]], channel_multiplier=-1).then_inc(s["sel_ready"], 1)
            g.memset(vpad[:, :, :, :, :], 0.0).then_inc(s["vz"], 1)

            def rstd1(b):
                q = b % 2
                pool.wait_ge(s["ve1_s"], b + 1)
                g.tensor_tensor(rs1[:, q, :], ve1[:, q, :], mhalf[:, 0:CH], ALU.pow).then_inc(s["rs1_s"], 1)

            def mask(b, n):
                G = 4 * b + n
                pool.wait_ge(s["probs_ready"], G + 1)
                a = probs[:, G % 4, :, 0:2 * P]
                g.affine_select(out=a, in_=a, compare_op=ALU.is_ge, fill=0.0, base=0,
                                pattern=[[0, 2], [0, 2], [1, P]], channel_multiplier=-1).then_inc(s["masked"], 1)

            def rstd2(b):
                pool.wait_ge(s["ve2_s"], b + 1)
                g.tensor_tensor(rs2[:, :], ve2[:, :], mhalf[:, 0:CH], ALU.pow).then_inc(s["rs2_s"], 1)

            def gated(b):
                pool.wait_ge(s["xa_ready"], b + 1)
                if b:
                    pool.wait_ge(s["y_ps"], b)
                g.tensor_tensor(z[:, :], xa[:, :], gate[:, b % 4, :], ALU.mult).then_inc(s["z_ready"], 1)

            pool.wait_ge(s["consts"], 1)
            for b in range(3):
                rstd1(b)
            for b in range(B + 1):
                if b < B:
                    mask(b, 0)
                if b >= 1:
                    rstd2(b - 1)
                if b < B:
                    mask(b, 1)
                    mask(b, 2)
                if b >= 1:
                    gated(b - 1)
                if b + 3 < B:
                    rstd1(b + 3)
                if b < B:
                    mask(b, 3)
            pool.wait_ge(s["ve3_s"], 1)
            g.tensor_tensor(rs3[:, :], ve3[:, :], mhalf[:, :], ALU.pow).then_inc(s["rs3_s"], 1)

        @block.scalar
        def _(act):
            a = nc.scalar
            act.wait_ge(s["tabs_ready"], 1)
            act.wait_ge(s["vz"], 1)

            def project(b):
                q = b % 2
                act.wait_ge(s["qk_ps"], b + 1)
                if b >= 2:
                    act.wait_ge(s["p3_s"], b - 1)
                for side in range(2):
                    a.activation(qk[:, q, side, :], PROJ[:, side * S:side * S + S], ACT.Silu,
                                 bias=b1_cols[:, 1 + side:2 + side]).then_inc(s["qk_ready"], 1)

            def gate_v(b):
                q = b % R
                act.wait_ge(s["gv_ps"], b + 1)
                if b >= R:
                    act.wait_ge(s["av_done"], 2 * (b - R + 1))
                    act.wait_ge(s["z_ready"], b - R + 1)
                a.activation(gate[:, b % 4, :], PROJ[:, 0:S], ACT.Silu, bias=b1_cols[:, 0:1]).then_inc(s["g_ready"], 1)
                src = PROJ[:, S:2 * S].rearrange("p (c j e r) -> p c j e r", c=CH, e=2, r=HD)
                for e in range(2):
                    a.activation(vpad[:, q, :, e::2, HD * e:HD * e + HD], src[:, :, :, e, :], ACT.Silu).then_inc(s["v_ready"], 1)

            def silu(b, n):
                G = 4 * b + n
                act.wait_ge(s["scores_ps"], G + 1)
                if G >= 4:
                    act.wait_ge(s["av_done"], G // 2 - 1)
                i = 2 * (G % 2)
                for k in range(2):
                    last = a.activation(probs[:, G % 4, k, :], bank[SCORE[i + k]][:, 0:SC], ACT.Silu, scale=HD ** -0.5)
                last.then_inc(s["probs_ready"], 1)

            def evac_o(b):
                act.wait_ge(s["av_done"], 2 * b + 2)
                if b:
                    act.wait_ge(s["o_ps"], b)
                a.activation(oT[:, :], OTB[:, 0:S], ACT.Copy).then_inc(s["ot_ready"], 1)

            def affine(b):
                act.wait_ge(s["xot_ps"], b + 1)
                if b:
                    act.wait_ge(s["z_ready"], b)
                a.activation(xa[:, :], OUTC[:, S:2 * S], ACT.Identity, scale=g_col, bias=b_col).then_inc(s["xa_ready"], 1)

            for b in range(2):
                project(b)
                gate_v(b)
            for b in range(B + 1):
                if b >= 1:
                    evac_o(b - 1)
                if b < B:
                    silu(b, 0)
                    silu(b, 1)
                if b + 2 < B:
                    project(b + 2)
                if b < B:
                    silu(b, 2)
                if b >= 1:
                    affine(b - 1)
                if b + 2 < B:
                    gate_v(b + 2)
                if b < B:
                    silu(b, 3)
            u = 0
            for e in range(E):
                for t in range(TM // TT):
                    act.wait_ge(s["hid_ps"], FC * (u + 1))
                    if u >= 2:
                        act.wait_ge(s["ye_ps"], (TT // P) * (u - 1))
                    for f in range(FC):
                        a.activation(hid[:, u % 2, f, :], bank[f][:, :], ACT.Gelu).then_inc(s["hid_ready"], 1)
                    u += 1

        @block.vector
        def _(dve):
            v = nc.vector
            v.memset(mhalf[:, :], -0.5).then_inc(s["consts"], 1)
            v.memset(tabT[:, :, :], 0.0).then_inc(s["tab0"], 1)
            v.memset(raw[:, 1:3, :], 0.0).then_inc(s["raw0"], 1)
            v.memset(ones_bf[:, :], 1.0)
            v.memset(zeroB[:, :], 0.0).then_inc(s["consts"], 1)
            dve.wait_ge(s["ids_in"], 16)
            for n, c in enumerate((40, 123, 91, 41, 125, 93)):
                v.tensor_scalar(cmpf[:, n, :], ids[:, :], float(c), None, ALU.is_equal)
            v.tensor_scalar(cmpf[:, 6, :], ids[:, :], 39990.0, None, ALU.is_gt).then_inc(s["cmp"], 1)
            dve.wait_ge(s["cmp"], 1)
            v.tensor_reduce(delta[:, :], cmpf[:, 0:3, :].rearrange("p n s -> p s n"), mybir.AxisListType.X, ALU.add).then_inc(s["del"], 1)
            v.tensor_reduce(nestf[:, :], cmpf[:, 3:6, :].rearrange("p n s -> p s n"), mybir.AxisListType.X, ALU.add).then_inc(s["del"], 1)
            dve.wait_ge(s["consts"], 2)
            v.tensor_tensor_scan(segf[:, :], cmpf[:, 6, :], zeroB[:, :], 0.0, ALU.add, ALU.add).then_inc(s["sgi"], 1)
            dve.wait_ge(s["del"], 2)
            v.tensor_tensor(delta[:, :], delta[:, :], nestf[:, :], ALU.subtract).then_inc(s["del"], 1)
            dve.wait_ge(s["sgi"], 1)
            v.tensor_copy(segi[:, :], segf[:, :]).then_inc(s["sgi"], 1)
            dve.wait_ge(s["del"], 3)
            v.tensor_tensor_scan(depth[:, :], delta[:, :], zeroB[:, :], 0.0, ALU.add, ALU.add).then_inc(s["dep"], 1)
            dve.wait_ge(s["sgi"], 2)
            v.tensor_scalar(segi8[:, :], segi[:, :], 7, None, ALU.bitwise_and).then_inc(s["sgi"], 1)
            dve.wait_ge(s["dep"], 1)
            v.tensor_tensor_scan(lowest[:, :], depth[:, :], zeroB[:, :], 0.0, ALU.min, ALU.min).then_inc(s["low"], 1)
            dve.wait_ge(s["low"], 1)
            v.tensor_tensor(nestf[:, :], depth[:, :], lowest[:, :], ALU.subtract).then_inc(s["nst"], 1)
            dve.wait_ge(s["nst"], 1)
            v.tensor_scalar(code[:, 0, :], nestf[:, :], 0.0, float(NEST - 1), ALU.max, ALU.min).then_inc(s["code_ready"], 1)
            dve.wait_ge(s["sgi"], 3)
            v.tensor_copy(code[:, 1, :], segi8[:, :]).then_inc(s["code_ready"], 1)
            dve.wait_ge(s["rows"], 1)
            v.tensor_scalar(row32[:, :], rowi[:, :], 31, None, ALU.bitwise_and).then_inc(s["idx_ready"], 1)
            dve.wait_ge(s["idx_ready"], 1)
            v.tensor_copy(rowf[:, :], row32[:, :]).then_inc(s["idx_ready"], 1)
            dve.wait_ge(s["idx_ready"], 2)
            v.tensor_scalar(rowge[:, :], rowf[:, :], 16.0, -16.0, ALU.is_ge, ALU.mult).then_inc(s["idx_ready"], 1)
            dve.wait_ge(s["idx_ready"], 3)
            v.tensor_tensor(rowcode[:, :], rowf[:, :], rowge[:, :], ALU.add).then_inc(s["idx_ready"], 1)
            dve.wait_ge(s["tr_ps"], 1)
            dve.wait_ge(s["tab0"], 1)
            for r in range(3):
                v.tensor_copy(tabT[:, 0, 32 * r:32 * r + NEST], XB[:, 0:NEST])
                v.tensor_copy(tabT[:, 1, 32 * r + 16:32 * r + 16 + SEG], XB[:, 16:16 + SEG])
            v.tensor_copy(cols6[:, :], XB[:, 24:30])
            v.tensor_copy(posT[:, :, :], XB[:, 256:512].rearrange("p (c n) -> p c n", c=CH)).then_inc(s["tabs_ready"], 1)
            dve.wait_ge(s["w1t_ps"], 1)
            v.tensor_copy(W1T[:, :, :], PROJ[:, :].rearrange("p (k n) -> p k n", k=4)).then_inc(s["w1t_ready"], 1)
            v.tensor_copy(W2T[:, :], OUTC[:, 0:D]).then_inc(s["w1t_ready"], 1)
            dve.wait_ge(s["pw_ps"], 1)
            v.tensor_copy(PW[:, :, :], XB[:, 0:256].rearrange("p (c n) -> p c n", c=CH)).then_inc(s["pw_ready"], 1)
            v.tensor_copy(raw[:, 0, :], XB[:, 256:256 + D]).then_inc(s["raw_ready"], 1)
            dve.wait_ge(s["raw_ready"], 1)
            dve.wait_ge(s["bias_in"], 96)
            v.tensor_copy(rhs_pieces[:, :, :], raw[:, :, :]).then_inc(s["pc1"], 1)
            dve.wait_ge(s["pc1"], 1)
            v.tensor_tensor(rest[:, :, :], raw[:, :, :], rhs_pieces[:, :, :], ALU.subtract).then_inc(s["pc2"], 1)
            dve.wait_ge(s["pc2"], 1)
            v.tensor_copy(rhs_pieces[32:64, :, :], rest[32:64, :, :])
            v.tensor_copy(piece2[64:96, :, :], rest[64:96, :, :]).then_inc(s["pc3"], 1)
            dve.wait_ge(s["pc3"], 1)
            v.tensor_tensor(rhs_pieces[64:96, :, :], rest[64:96, :, :], piece2[64:96, :, :], ALU.subtract)
            v.memset(rhs_pieces[96:128, :, :], 0.0).then_inc(s["pieces_ready"], 1)
            dve.wait_ge(s["idx_ready"], 4)
            for n in range(B // 2):
                dve.wait_ge(s["code_ps"], n + 1)
                v.tensor_scalar(onehot[:, 2 * n:2 * n + 2, :], bank[SCORE[n]][:, :].rearrange("p (b s) -> p b s", b=2),
                                rowcode[:, 0:1], None, ALU.is_equal).then_inc(s["onehot_ready"], 1)

            def embed(b):
                q = b % 2
                hb = h_all[:, CH * b:CH * b + CH, :]
                dve.wait_ge(s["embed_ps"], b + 1)
                v.tensor_tensor(hb, XB[:, 0:S].rearrange("p (c n) -> p c n", c=CH), PW[:, :, :], ALU.add).then_inc(s["h_ready"], 1)
                dve.wait_ge(s["h_ready"], b + 1)
                for c in range(CH):
                    v.bn_stats(bst[:, q, c, :], h_all[:, CH * b + c, :]).then_inc(s["st1"], 1)
                for c in range(CH):
                    dve.wait_ge(s["st1"], CH * b + c + 1)
                    v.bn_aggr(mv1[:, q, c, :], bst[:, q, c, :]).then_inc(s["mv1_s"], 1)
                dve.wait_ge(s["mv1_s"], CH * (b + 1))
                v.tensor_scalar(ve1[:, q, :], mv1[:, q, :, 1], EPS, None, ALU.add).then_inc(s["ve1_s"], 1)

            def normalise(b):
                q = b % 2
                dve.wait_ge(s["rs1_s"], b + 1)
                if b >= 2:
                    dve.wait_ge(s["xt_ps"], b - 1)
                for c in range(CH):
                    v.tensor_scalar(xn[:, q, c, :], h_all[:, CH * b + c, :], mv1[:, q, c, 0:1], rs1[:, q, c:c + 1],
                                    ALU.subtract, ALU.mult).then_inc(s["xn_ready"], 1)

            def evac_x(b):
                dve.wait_ge(s["xt_ps"], b + 1)
                if b >= 2:
                    dve.wait_ge(s["gv_ps"], b - 1)
                v.tensor_copy(xT[:, b % 2, :], XB[:, S:2 * S]).then_inc(s["xt_ready"], 1)

            def split(b):
                q = b % 2
                dve.wait_ge(s["qk_ready"], 2 * (b + 1))
                if b >= 2:
                    for done in bounced:
                        dve.wait_ge(done, 16 * (b - 1))
                v.tensor_copy(qkp[0][:, q, :, :], qk[:, q, :, :]).then_inc(s["p1_s"], 1)
                dve.wait_ge(s["p1_s"], b + 1)
                v.tensor_tensor(qkr[:, q, :, :], qk[:, q, :, :], qkp[0][:, q, :, :], ALU.subtract).then_inc(s["r1_s"], 1)
                dve.wait_ge(s["r1_s"], b + 1)
                v.tensor_copy(qkp[1][:, q, :, :], qkr[:, q, :, :]).then_inc(s["p2_s"], 1)
                dve.wait_ge(s["p2_s"], b + 1)
                v.tensor_tensor(qkp[2][:, q, :, :], qkr[:, q, :, :], qkp[1][:, q, :, :], ALU.subtract).then_inc(s["p3_s"], 1)

            def stats2(b):
                dve.wait_ge(s["o_ps"], b + 1)
                for c in range(CH):
                    v.bn_stats(bst2[:, c, :], OUTC[:, P * c:P * c + P]).then_inc(s["st2"], 1)
                for c in range(CH):
                    dve.wait_ge(s["st2"], CH * b + c + 1)
                    v.bn_aggr(mv2[:, c, :], bst2[:, c, :]).then_inc(s["mv2_s"], 1)
                dve.wait_ge(s["mv2_s"], CH * (b + 1))
                v.tensor_scalar(ve2[:, :], mv2[:, :, 1], EPS, None, ALU.add).then_inc(s["ve2_s"], 1)

            def normalise2(b):
                dve.wait_ge(s["rs2_s"], b + 1)
                if b:
                    dve.wait_ge(s["xot_ps"], b)
                for c in range(CH):
                    v.tensor_scalar(xo[:, c, :], OUTC[:, P * c:P * c + P], mv2[:, c, 0:1], rs2[:, c:c + 1],
                                    ALU.subtract, ALU.mult).then_inc(s["xo_ready"], 1)

            def residual(b):
                hb = h_all[:, CH * b:CH * b + CH, :]
                dve.wait_ge(s["y_ps"], b + 1)
                v.tensor_tensor(hb, OUTC[:, 0:S].rearrange("p (c n) -> p c n", c=CH), hb, ALU.add).then_inc(s["h2_ready"], 1)

            embed(0)
            normalise(0)
            evac_x(0)
            embed(1)
            split(0)
            normalise(1)
            evac_x(1)
            embed(2)
            split(1)
            for b in range(B + 1):
                if b + 2 < B:
                    normalise(b + 2)
                    evac_x(b + 2)
                if b >= 1:
                    stats2(b - 1)
                if b + 2 < B:
                    split(b + 2)
                if b >= 1:
                    normalise2(b - 1)
                if b + 3 < B:
                    embed(b + 3)
                if b >= 1:
                    residual(b - 1)

            dve.wait_ge(s["rts_in"], 32)
            v.tensor_copy(re_f[:, :, :], re_i[:, :, :]).then_inc(s["cf0"], 1)
            dve.wait_ge(s["cf0"], 1)
            for e in range(E):
                for k in range(2):
                    v.scalar_tensor_tensor(coef[:, k, e, :], re_f[:, :, k], float(e), rw[:, :, k], ALU.is_equal, ALU.mult).then_inc(s["cf1"], 1)
            dve.wait_ge(s["cf1"], 2 * E)
            v.tensor_tensor(coefs[:, :, :], coef[:, 0, :, :], coef[:, 1, :, :], ALU.add).then_inc(s["coef_ready"], 1)
            dve.wait_ge(s["h2_ready"], TM // S)
            for c in range(MC):
                v.bn_stats(bst3[:, c, :], h_all[:, c, :]).then_inc(s["st3"], 1)
            for c in range(MC):
                dve.wait_ge(s["st3"], c + 1)
                v.bn_aggr(mv3[:, c, :], bst3[:, c, :]).then_inc(s["mv3_s"], 1)
            dve.wait_ge(s["mv3_s"], MC)
            v.tensor_scalar(ve3[:, :], mv3[:, :, 1], EPS, None, ALU.add).then_inc(s["ve3_s"], 1)
            dve.wait_ge(s["rs3_s"], 1)
            for c in range(MC):
                v.tensor_scalar(xm[:, c, :], h_all[:, c, :], mv3[:, c, 0:1], rs3[:, c:c + 1],
                                ALU.subtract, ALU.mult).then_inc(s["xm_ready"], 1)
            for n in range(2):
                dve.wait_ge(s["xmt_ps"], n + 1)
                v.tensor_copy(xmT[:, TT * n:TT * n + TT], bank[4 + n][:, :]).then_inc(s["xmt_ready"], 1)
            dve.wait_ge(s["coef_ready"], 1)
            n = 0
            for e in range(E):
                for c in range(MC):
                    dve.wait_ge(s["ye_ps"], n + 1)
                    if e:
                        dve.wait_ge(s["acc_ready"], n + 1 - MC)
                    v.scalar_tensor_tensor(h_all[:, c, :], bank[4 + n % 4][:, 0:D], coefs[:, e, c:c + 1], h_all[:, c, :],
                                           ALU.mult, ALU.add).then_inc(s["acc_ready"], 1)
                    n += 1

        @block.tensor
        def _(pe):
            mm = nc.tensor.matmul
            tr = nc.tensor.transpose
            pe.wait_ge(s["ident_ready"], 1)
            pe.wait_ge(s["small_in"], 48)
            pe.wait_ge(s["pos_in"], 16)
            tr(XB[:, 0:NEST], nest_sb[:, :], ident[0:NEST, 0:NEST])
            tr(XB[:, 16:16 + SEG], seg_sb[:, :], ident[0:SEG, 0:SEG])
            pe.wait_ge(s["cols_in"], 48)
            tr(XB[:, 24:30], rows6[:, :], ident[0:6, 0:6])
            for c in range(CH):
                last = tr(XB[:, 256 + P * c:256 + P * c + P], pos_sb[:, c, :], ident[:, :])
            last.then_inc(s["tr_ps"], 1)
            pe.wait_ge(s["attnw_in"], 32)
            for k in range(4):
                tr(PROJ[:, P * k:P * k + P], W1_sb[:, k, :], ident[:, :])
            tr(OUTC[:, 0:D], W2_sb[:, :], ident[:, :]).then_inc(s["w1t_ps"], 1)
            pe.wait_ge(s["tabs_ready"], 1)
            for c in range(CH):
                mm(XB[:, P * c:P * c + P], posT[:, c, :], tokW_sb[:, 0, :], start=True, stop=True)
            mm(XB[:, 256:256 + D], tabT[:, 0, :], tokW_sb[:, 1, :], start=True, stop=False)
            mm(XB[:, 256:256 + D], tabT[:, 1, :], tokW_sb[:, 2, :], start=False, stop=True).then_inc(s["pw_ps"], 1)
            pe.wait_ge(s["code_ready"], 2)
            pe.wait_ge(s["sel_ready"], 2)
            for n in range(B // 2):
                for b in (2 * n, 2 * n + 1):
                    dst = bank[SCORE[n]][:, S * (b % 2):S * (b % 2) + S]
                    mm(dst, sel[:, 0, b, :], code[:, 0, :], start=True, stop=False)
                    last = mm(dst, sel[:, 1, b, :], code[:, 1, :], start=False, stop=True)
                last.then_inc(s["code_ps"], 1)

            def embed(b):
                pe.wait_ge(s["onehot_ready"], b // 2 + 1)
                if b == 0:
                    pe.wait_ge(s["pieces_ready"], 1)
                if b >= 1:
                    pe.wait_ge(s["xt_ready"], b)
                    pe.wait_ge(s["h_ready"], b)
                for c in range(CH):
                    last = mm(XB[:, P * c:P * c + P], onehot[:, b, P * c:P * c + P], rhs_pieces[:, 0, :], start=True, stop=True)
                last.then_inc(s["embed_ps"], 1)

            def transpose_x(b):
                pe.wait_ge(s["xn_ready"], CH * (b + 1))
                pe.wait_ge(s["h_ready"], b + 1)
                for c in range(CH):
                    last = tr(XB[:, S + P * c:S + P * c + P], xn[:, b % 2, c, :], ident[:, :])
                last.then_inc(s["xt_ps"], 1)

            def project_qk(b):
                pe.wait_ge(s["xt_ready"], b + 1)
                if b == 0:
                    pe.wait_ge(s["w1t_ready"], 2)
                if b:
                    pe.wait_ge(s["v_ready"], 2 * b)
                for side in range(2):
                    last = mm(PROJ[:, side * S:side * S + S], W1T[:, 1 + side, :], xT[:, b % 2, :], start=True, stop=True)
                last.then_inc(s["qk_ps"], 1)

            def project_gv(b):
                pe.wait_ge(s["qk_ready"], 2 * (b + 1))
                mm(PROJ[:, 0:S], W1T[:, 0, :], xT[:, b % 2, :], start=True, stop=True)
                for c in range(CH):
                    dst = PROJ[:, S + P * c:S + P * c + P]
                    mm(dst, xT[:, b % 2, P * c:P * c + P], W1T[:, 3, :], start=True, stop=False)
                    last = mm(dst, ones_bf[:, :], rhs_pieces[:, 1, :], start=False, stop=True)
                last.then_inc(s["gv_ps"], 1)

            def scores(b, n):
                G, q = 4 * b + n, b % R
                if n == 0:
                    pe.wait_ge(stk[q], 16 * NDMA * (b // R + 1))
                if G >= 2:
                    pe.wait_ge(s["probs_ready"], G - 1)
                i = 2 * (G % 2)
                for k, h in enumerate(HALVES[n // 2][2 * (n % 2):2 * (n % 2) + 2]):
                    dst, kk, qq = bank[SCORE[i + k]], stacks[:, q, 1, h, :], stacks[:, q, 0, h, :]
                    mm(dst[:, P:SC], kk[:, 0:P], qq, start=True, stop=True)
                    last = mm(dst[:, 0:P], kk[:, P:S], qq[:, P:S], start=True, stop=True)
                last.then_inc(s["scores_ps"], 1)

            def attend(b, half):
                q = b % R
                pe.wait_ge(s["masked"], 4 * b + 2 * half + 2)
                if half == 0:
                    pe.wait_ge(s["v_ready"], 2 * (b + 1))
                    if b:
                        pe.wait_ge(s["ot_ready"], b)
                for c in range(CH):
                    for j, h in enumerate(HALVES[half]):
                        pr = probs[:, (2 * half + j // 2) % 4, j % 2, :]
                        dst = OTB[32 * j:32 * j + 32, P * c:S]
                        last = mm(dst, vpad[:, q, c, h, :], pr[:, P:SC] if c == 0 else pr[:, 0:P],
                                  start=(half == 0 and c == 0), stop=(half == 1 and c == 1), skip_group_check=True)
                last.then_inc(s["av_done"], 1)

            def transpose_o(b):
                pe.wait_ge(s["ot_ready"], b + 1)
                if b:
                    pe.wait_ge(s["h2_ready"], b)
                for c in range(CH):
                    last = tr(OUTC[:, P * c:P * c + P], oT[:, P * c:P * c + P], ident[:, :])
                last.then_inc(s["o_ps"], 1)

            def transpose_xo(b):
                pe.wait_ge(s["xo_ready"], CH * (b + 1))
                for c in range(CH):
                    last = tr(OUTC[:, S + P * c:S + P * c + P], xo[:, c, :], ident[:, :])
                last.then_inc(s["xot_ps"], 1)

            def out_proj(b):
                pe.wait_ge(s["z_ready"], b + 1)
                for c in range(CH):
                    dst = OUTC[:, P * c:P * c + P]
                    mm(dst, z[:, P * c:P * c + P], W2T[:, :], start=True, stop=False)
                    last = mm(dst, ones_bf[:, :], rhs_pieces[:, 2, :], start=False, stop=True)
                last.then_inc(s["y_ps"], 1)

            pe.wait_ge(s["pw_ready"], 1)
            pe.wait_ge(s["raw_ready"], 1)
            embed(0)
            transpose_x(0)
            embed(1)
            project_qk(0)
            project_gv(0)
            transpose_x(1)
            embed(2)
            project_qk(1)
            project_gv(1)
            pe.wait_ge(s["onehot_ready"], 4)
            for b in range(B + 1):
                if b < B:
                    scores(b, 0)
                    scores(b, 1)
                if b + 2 < B:
                    transpose_x(b + 2)
                    project_qk(b + 2)
                if b >= 1:
                    transpose_o(b - 1)
                if b < B:
                    scores(b, 2)
                    attend(b, 0)
                if b + 2 < B:
                    project_gv(b + 2)
                if b >= 1:
                    transpose_xo(b - 1)
                if b < B:
                    scores(b, 3)
                if b + 3 < B:
                    embed(b + 3)
                if b >= 1:
                    out_proj(b - 1)
                if b < B:
                    attend(b, 1)

            pe.wait_ge(s["h2_ready"], B)
            for n in range(2):
                for c in range(4):
                    pe.wait_ge(s["xm_ready"], 4 * n + c + 1)
                    last = tr(bank[4 + n][:, P * c:P * c + P], xm[:, 4 * n + c, :], ident[:, :])
                last.then_inc(s["xmt_ps"], 1)
            pe.wait_ge(s["w1_in"], 16)
            pe.wait_ge(s["w2_in"], 16)
            units = [(e, t) for e in range(E) for t in range(TM // TT)]

            def up(u):
                e, t = units[u]
                if e == 0:
                    pe.wait_ge(s["xmt_ready"], t + 1)
                for f in range(FC):
                    if u:
                        pe.wait_ge(s["hid_ready"], FC * (u - 1) + f + 1)
                    mm(bank[f][:, :], w1_sb[:, e, P * f:P * f + P], xmT[:, TT * t:TT * t + TT], start=True, stop=True).then_inc(s["hid_ps"], 1)

            def down(u):
                e, t = units[u]
                pe.wait_ge(s["hid_ready"], FC * (u + 1))
                if u == 0:
                    pe.wait_ge(s["xmt_ready"], 2)
                for c in range(TT // P):
                    n = 4 * u + c
                    if n >= 4:
                        pe.wait_ge(s["acc_ready"], n - 3)
                    for f in range(FC):
                        last = mm(bank[4 + n % 4][:, 0:D], hid[:, u % 2, f, P * c:P * c + P], w2_sb[:, e, f, :],
                                  start=(f == 0), stop=(f == FC - 1))
                    last.then_inc(s["ye_ps"], 1)

            up(0)
            for u in range(len(units)):
                if u + 1 < len(units):
                    up(u + 1)
                down(u)


_INS = ["x", "L0_tok_pos_table", "L0_tok_nest_table", "L0_tok_seg_table", "L0_tok_W", "L0_attn_W1", "L0_attn_b1",
        "L0_attn_ln_g", "L0_attn_ln_b", "L0_attn_W2", "L0_attn_b2", "L0_ffn_expert_weights", "L0_ffn_expert_indices",
        "L0_ffn_w1", "L0_ffn_w2"]


def kernel(**inputs):
    import numpy as np
    import concourse.bacc as bacc
    from concourse import mybir
    from concourse.bass_utils import run_bass_kernel_spmd

    nc = bacc.Bacc("TRN2", target_bir_lowering=False, num_devices=1)
    arrays, args = {}, []
    for name in _INS:
        a = np.ascontiguousarray(inputs[name])
        arrays[f"in_{name}"] = a
        args.append(nc.dram_tensor(f"in_{name}", a.shape, mybir.dt.from_np(a.dtype), kind="ExternalInput").ap())
    out = nc.dram_tensor("out", (8, 256, 128), mybir.dt.float32, kind="ExternalOutput").ap()
    build(nc, *args, out)
    r = run_bass_kernel_spmd(nc, [arrays], core_ids=[0])
    return r.results[0]["out"]
```

```python
import concourse.bass as bass
from concourse import mybir
from contextlib import ExitStack

F32, BF16, I32 = mybir.dt.float32, mybir.dt.bfloat16, mybir.dt.int32
ALU = mybir.AluOpType
ACT = mybir.ActivationFunctionType

P = 128
B, S, D = 8, 256, 128
CH = S // P
NC = B * CH
H, HD = 8, 16
NEST, SEG = 16, 8
PIECES = ((0, 0), (0, 1), (1, 0), (0, 2), (1, 1), (2, 0))
KS = HD * len(PIECES)
SC = S + P
HALVES = ((0, 2, 4, 6), (1, 3, 5, 7))
E, FF = 8, 512
FC = FF // P
TM = 1024
MC = TM // P
TOPK = 2
NA = TM * TOPK
NB = (NA + E * (P - 1)) // P
ROW = D + 2
NOBODY = 1 << 20
EPS = 1e-5
PR = 8
R = 4


def build(nc, x, pos_table, nest_table, seg_table, tok_W, W1, b1, ln_g, ln_b, W2, b2, route_w, route_e, w1, w2, out):
    ctx = ExitStack()
    with ctx:
        def sb(name, shape, dt=F32):
            return ctx.enter_context(nc.sbuf_tensor(name, shape, dt))

        def pb(name):
            return ctx.enter_context(nc.psum_tensor(name, [P, 512], F32))

        def sem(name):
            return ctx.enter_context(nc.semaphore(name))

        ident = sb("ident", [P, P])
        ids = sb("ids", [B, S], I32)
        nest_sb = sb("nest_sb", [NEST, D])
        seg_sb = sb("seg_sb", [SEG, D])
        tokW_sb = sb("tokW_sb", [P, 3, D])
        pos_sb = sb("pos_sb", [P, CH, D])
        W1_sb = sb("W1_sb", [P, 4, D])
        W2_sb = sb("W2_sb", [P, D])
        rows6 = sb("rows6", [6, P])
        cols6 = sb("cols6", [P, 6])
        b1_cols, g_col, b_col = cols6[:, 0:4], cols6[:, 4:5], cols6[:, 5:6]
        W1T = sb("W1T", [P, 4, P])
        W2T = sb("W2T", [P, D])
        posT = sb("posT", [P, CH, P])
        tabT = sb("tabT", [P, 2, P])
        PW = sb("PW", [P, CH, D])
        raw = sb("raw", [P, 3, D])
        rest = sb("rest", [P, 3, D])
        piece2 = sb("piece2", [P, 3, D], BF16)
        rhs_pieces = sb("rhs_pieces", [P, 3, D], BF16)
        ones_bf = sb("ones_bf", [P, P], BF16)
        cmpf = sb("cmpf", [B, 7, S])
        delta = sb("delta", [B, S])
        depth = sb("depth", [B, S])
        lowest = sb("lowest", [B, S])
        nestf = sb("nestf", [B, S])
        segf = sb("segf", [B, S])
        segi = sb("segi", [B, S], I32)
        segi8 = sb("segi8", [B, S], I32)
        zeroB = sb("zeroB", [B, S])
        code = sb("code", [B, 2, S], BF16)
        sel = sb("sel", [B, 2, B, P], BF16)
        rowi = sb("rowi", [P, 1], I32)
        row32 = sb("row32", [P, 1], I32)
        rowf = sb("rowf", [P, 1])
        rowge = sb("rowge", [P, 1])
        rowcode = sb("rowcode", [P, 1])
        onehot = sb("onehot", [P, B, S], BF16)
        h_all = sb("h_all", [P, NC, D])
        bst = sb("bst", [P, 2, CH, 6])
        mv1 = sb("mv1", [P, 2, CH, 2])
        ve1 = sb("ve1", [P, 2, CH])
        rs1 = sb("rs1", [P, 2, CH])
        mhalf = sb("mhalf", [P, MC])
        xn = sb("xn", [P, 2, CH, D])
        xT = sb("xT", [P, 2, S])
        qk = sb("qk", [P, 2, 2, S])
        qkp = [sb(f"qkp{i}", [P, 2, 2, S], BF16) for i in range(3)]
        qkr = sb("qkr", [P, 2, 2, S])
        stacks = sb("stacks", [KS, R, 2, H, S], BF16)
        bounce = nc.dram_tensor("bounce", (2, 3, P, 2, S), BF16, kind="Internal").ap()
        gate = sb("gate", [P, R, S])
        vpad = sb("vpad", [P, R, CH, H, 32])
        probs = sb("probs", [P, PR, 2, SC])
        oT = sb("oT", [P, S])
        bst2 = sb("bst2", [P, CH, 6])
        mv2 = sb("mv2", [P, CH, 2])
        ve2 = sb("ve2", [P, CH])
        rs2 = sb("rs2", [P, CH])
        xo = sb("xo", [P, CH, D])
        xa = sb("xa", [P, S])
        z = sb("z", [P, S])
        upper = sb("upper", [P, P], BF16)
        re_i = sb("re_i", [P, MC, TOPK], I32)
        re_f = sb("re_f", [P, MC * TOPK])
        rw = sb("rw", [P, MC, TOPK])
        chosen = sb("chosen", [P, E, MC * TOPK])
        restart = sb("restart", [P, E, MC * TOPK])
        rank = sb("rank", [P, E, MC * TOPK])
        count_bf = sb("count_bf", [P, E], BF16)
        zeros8 = sb("zeros8", [P, E])
        prefix = sb("prefix", [P, 2, E])
        full_i = sb("full_i", [P, E], I32)
        blocks_i = sb("blocks_i", [P, E], I32)
        blocks = sb("blocks", [P, E])
        ends = sb("ends", [P, E])
        starts = sb("starts", [P, E])
        offset = sb("offset", [P, E])
        place = sb("place", [P, E, MC * TOPK])
        placed = sb("placed", [P, E, MC * TOPK])
        slot_f = sb("slot_f", [P, MC * TOPK])
        slot = sb("slot", [P, MC * TOPK], I32)
        block_no = sb("block_no", [P, NB, E])
        passed = sb("passed", [P, NB, E])
        owner_f = sb("owner_f", [P, NB])
        owner7 = sb("owner7", [P, NB])
        owner = sb("owner", [P, NB], I32)
        bst3 = sb("bst3", [P, MC, 6])
        mv3 = sb("mv3", [P, MC, 2])
        ve3 = sb("ve3", [P, MC])
        rs3 = sb("rs3", [P, MC])
        xrow = sb("xrow", [P, MC, TOPK, ROW])
        xb = sb("xb", [P, NB, ROW])
        xbT = sb("xbT", [P, NB * P])
        w1s = [sb(f"w1s{i}", [P, FF]) for i in range(2)]
        w2_sb = sb("w2_sb", [P, E * FC * D])
        hid = [sb(f"hid{i}", [P, FF]) for i in range(2)]
        yw = [sb(f"yw{i}", [P, D]) for i in range(2)]
        spent = probs[:, :, :, :].rearrange("p g a n -> p (g a n)")
        yb = spent[:, 0:NA // P * D].rearrange("p (c k d) -> p c k d", k=TOPK, d=D)
        ysum = spent[:, NA // P * D:NA // P * D + MC * D].rearrange("p (c d) -> p c d", d=D)
        slots_dram = nc.dram_tensor("slots_dram", (NB * P, ROW), F32, kind="Internal").ap()
        y_dram = nc.dram_tensor("y_dram", (NA, D), F32, kind="Internal").ap()

        bank = [pb(f"bank{i}") for i in range(8)]
        SCORE, PROJ, OUTC, OTB, XB = (0, 1, 2, 3), bank[4], bank[5], bank[6], bank[7]

        names = """ids_in small_in cols_in attnw_in bias_in pos_in rts_in w2_in ident0 ident_ready sel0 sel_ready upper0 upper_ready
        consts rows idx_ready o_cnt c_cnt del dep low nst sgi sgf code_ready tab0 tr_ps tabs_ready w1t_ps w1t_ready pw_ps pw_ready raw0 raw_ready
        pc1 pc2 pc3 pieces_ready code_ps onehot_ready embed_ps h_ready st1 mv1_s ve1_s rs1_s xn_ready xt_ps xt_ready
        qk_ps qk_ready gv_ps g_ready v_ready p1_s r1_s p2_s p3_s scores_ps probs_ready masked av_done ot_ready o_ps st2 mv2_s ve2_s rs2_s
        xo_ready xot_ps xa_ready z_ready y_ps h2_ready stored vz
        e_f chosen_s restart_s ranked counted prefix_ps prefix_ready rnd blocks_s slots_ready owner_ready
        xb0 slots_cleared rows_meta st3 mv3_s ve3_s rs3_s xm_ready scattered xb_in xbt_ps xbt_ready
        hid_ps hid_ready ye_ps yw_ready y_stored yb_in ysum_ready out_ready"""
        s = {n: sem(n) for n in names.split()}
        w1_in = [sem("w1_in_even"), sem("w1_in_odd")]
        y_out = [sem("y_out_even"), sem("y_out_odd")]
        stk = [sem(f"stacks_in{i}") for i in range(R)]
        bounced = [sem(f"bounced{i}") for i in range(3)]
        NDMA = 2 * len(PIECES)
        block = ctx.enter_context(nc.Block())

        @block.sync
        def _(sp):
            sp.dma_start(ids[:, :], x).then_inc(s["ids_in"], 16)
            sp.dma_start(nest_sb[:, :], nest_table).then_inc(s["small_in"], 16)
            sp.dma_start(seg_sb[:, :], seg_table).then_inc(s["small_in"], 16)
            sp.dma_start(tokW_sb[:, :, :], tok_W.rearrange("(k p) n -> p k n", p=P)).then_inc(s["small_in"], 16)
            sp.dma_start(pos_sb[:, :, :], pos_table[0:S, :].rearrange("(c p) n -> p c n", p=P)).then_inc(s["pos_in"], 16)
            sp.dma_start(W1_sb[:, :, :], W1.rearrange("(k p) n -> p k n", p=P)).then_inc(s["attnw_in"], 16)
            sp.dma_start(W2_sb[:, :], W2).then_inc(s["attnw_in"], 16)
            sp.dma_start(rows6[0:4, :], b1.rearrange("(k p) -> k p", p=P)).then_inc(s["cols_in"], 16)
            sp.dma_start(rows6[4:5, :], ln_g.rearrange("(a p) -> a p", a=1)).then_inc(s["cols_in"], 16)
            sp.dma_start(rows6[5:6, :], ln_b.rearrange("(a p) -> a p", a=1)).then_inc(s["cols_in"], 16)
            sp.wait_ge(s["raw0"], 1)
            for r in range(3):
                sp.dma_start(raw[32 * r:32 * r + 1, 1, :], b1[3 * P:4 * P].rearrange("(a n) -> a n", a=1)).then_inc(s["bias_in"], 16)
                sp.dma_start(raw[32 * r:32 * r + 1, 2, :], b2.rearrange("(a n) -> a n", a=1)).then_inc(s["bias_in"], 16)
            sp.dma_start(re_i[:, :, :], route_e.rearrange("(c p) k -> p c k", p=P)).then_inc(s["rts_in"], 16)
            sp.dma_start(rw[:, :, :], route_w.rearrange("(c p) k -> p c k", p=P)).then_inc(s["rts_in"], 16)

            def stack(b):
                q = b % 2
                if b >= 2:
                    sp.wait_ge(stk[(b - 2) % R], 16 * NDMA * ((b - 2) // R + 1))
                for piece in range(3):
                    sp.wait_ge(s[("p1_s", "p2_s", "p3_s")[piece]], b + 1)
                    sp.dma_start(bounce[q, piece], qkp[piece][:, q, :, :]).then_inc(bounced[piece], 16)
                if b >= R:
                    sp.wait_ge(s["scores_ps"], 4 * (b - R + 1))
                for piece in range(3):
                    sp.wait_ge(bounced[piece], 16 * (b + 1))
                    for slot, pair in enumerate(PIECES):
                        for side in range(2):
                            if pair[side] == piece:
                                sp.dma_start(stacks[HD * slot:HD * (slot + 1), b % R, side, :, :],
                                             bounce[q, piece, :, side, :].rearrange("(h r) s -> r h s", r=HD)).then_inc(stk[b % R], 16)

            def store(b):
                sp.wait_ge(s["h2_ready"], b + 1)
                sp.dma_start(out[b].rearrange("(c p) d -> p c d", p=P), h_all[:, CH * b:CH * b + CH, :]).then_inc(s["stored"], 16)

            sp.wait_ge(s["xb0"], 2)
            sp.dma_start(slots_dram.rearrange("(i p) n -> p i n", p=P), xb[:, :, :]).then_inc(s["slots_cleared"], 16)
            stack(0)
            stack(1)
            sp.dma_start(w2_sb[:, :].rearrange("p (g d) -> p g d", d=D), w2.rearrange("e (c p) d -> p (e c) d", p=P)).then_inc(s["w2_in"], 16)
            for b in range(2, B):
                stack(b)
            for b in range(TM // S, B):
                store(b)

            def stage(i, q, first):
                if not first:
                    sp.wait_ge(s["hid_ps"], i - 1)
                e = sp.value_load(owner[0:1, bass.ds(i, 1)], min_val=0, max_val=E - 1)
                sp.dma_start(w1s[q][:, :], w1[bass.ds(e, 1)].rearrange("a p f -> (a p) f")).then_inc(w1_in[q], 16)

            sp.wait_ge(s["owner_ready"], 1)
            stage(0, 0, True)
            stage(1, 1, True)
            sp.wait_ge(s["scattered"], 16 * MC * TOPK)
            for n in range(0, NB, 4):
                m = min(4, NB - n)
                sp.dma_start(xb[:, n:n + m, :], slots_dram[P * n:P * (n + m), :].rearrange("(i p) n -> p i n", p=P)).then_inc(s["xb_in"], 16)
                sp.wait_ge(s["xb_in"], 16 * (n // 4 + 1))
            with sp.Fori(2, NB - 2, 2) as i:
                stage(i, 0, False)
                stage(i + 1, 1, False)
            if NB % 2:
                stage(NB - 1, (NB - 1) % 2, False)

            for q in range(2):
                sp.wait_ge(y_out[q], 16 * ((NB + 1 - q) // 2))
            for n in range(0, MC, 2):
                sp.dma_start(yb[:, n:n + 2, :, :], y_dram[TOPK * P * n:TOPK * P * (n + 2), :].rearrange("(c p k) d -> p c k d", p=P, k=TOPK)).then_inc(s["yb_in"], 16)
                sp.wait_ge(s["yb_in"], 16 * (n // 2 + 1))
            for n in range(0, MC, 2):
                sp.wait_ge(s["out_ready"], n // 2 + 1)
                sp.dma_start(out[n // 2].rearrange("(c p) d -> p c d", p=P), ysum[:, n:n + 2, :]).then_inc(s["stored"], 16)
            sp.wait_ge(s["stored"], 16 * B)

        @block.gpsimd
        def _(pool):
            g = nc.gpsimd
            g.memset(ident[:, :], 0.0).then_inc(s["ident0"], 1)
            g.memset(sel[:, :, :, :], 0.0).then_inc(s["sel0"], 1)
            g.memset(upper[:, :], 1.0).then_inc(s["upper0"], 1)
            pool.wait_ge(s["ident0"], 1)
            g.affine_select(out=ident[:, :], in_=ident[:, :], compare_op=ALU.not_equal, fill=1.0, base=0,
                            pattern=[[-1, P]], channel_multiplier=1).then_inc(s["ident_ready"], 1)
            g.iota(rowi[:, :], pattern=[[0, 1]], base=0, channel_multiplier=1).then_inc(s["rows"], 1)
            pool.wait_ge(s["sel0"], 1)
            v = sel[:, :, :, :].rearrange("k t b (q r) -> k t b q r", r=32)
            for t in range(2):
                for r in range(3):
                    g.memset(v[:, t, :, r, 16 * t:16 * t + (NEST, SEG)[t]], 1.0).then_inc(s["sel0"], 1)
            pool.wait_ge(s["sel0"], 7)
            for t in range(2):
                g.affine_select(out=sel[:, t, :, :], in_=sel[:, t, :, :], compare_op=ALU.is_equal, fill=0.0, base=0,
                                pattern=[[1, B], [0, P]], channel_multiplier=-1).then_inc(s["sel_ready"], 1)
            g.memset(vpad[:, :, :, :, :], 0.0).then_inc(s["vz"], 1)
            pool.wait_ge(s["upper0"], 1)
            g.affine_select(out=upper[:, :], in_=upper[:, :], compare_op=ALU.is_gt, fill=0.0, base=0,
                            pattern=[[1, P]], channel_multiplier=-1).then_inc(s["upper_ready"], 1)
            g.memset(xb[:, :, :], 0.0).then_inc(s["xb0"], 1)
            pool.wait_ge(s["xb0"], 1)
            g.memset(xb[:, :, D:D + 1].bitcast(I32), NOBODY).then_inc(s["xb0"], 1)
            g.iota(block_no[:, :, :], pattern=[[1, NB], [0, E]], base=0, channel_multiplier=0, allow_small_or_imprecise_dtypes=True).then_inc(s["rows"], 1)
            g.iota(xrow[:, :, :, D:D + 1].bitcast(I32), pattern=[[TOPK * P, MC], [1, TOPK], [0, 1]], base=0, channel_multiplier=TOPK).then_inc(s["rows_meta"], 1)
            pool.wait_ge(s["rts_in"], 32)
            g.tensor_copy(xrow[:, :, :, D + 1:D + 2], rw[:, :, :]).then_inc(s["rows_meta"], 1)

            def rstd1(b):
                q = b % 2
                pool.wait_ge(s["ve1_s"], b + 1)
                g.tensor_tensor(rs1[:, q, :], ve1[:, q, :], mhalf[:, 0:CH], ALU.pow).then_inc(s["rs1_s"], 1)

            def mask(b, n):
                G = 4 * b + n
                pool.wait_ge(s["probs_ready"], G + 1)
                a = probs[:, G % PR, :, 0:2 * P]
                g.affine_select(out=a, in_=a, compare_op=ALU.is_ge, fill=0.0, base=0,
                                pattern=[[0, 2], [0, 2], [1, P]], channel_multiplier=-1).then_inc(s["masked"], 1)

            def rstd2(b):
                pool.wait_ge(s["ve2_s"], b + 1)
                g.tensor_tensor(rs2[:, :], ve2[:, :], mhalf[:, 0:CH], ALU.pow).then_inc(s["rs2_s"], 1)

            def gated(b):
                pool.wait_ge(s["xa_ready"], b + 1)
                if b:
                    pool.wait_ge(s["y_ps"], b)
                g.tensor_tensor(z[:, :], xa[:, :], gate[:, b % R, :], ALU.mult).then_inc(s["z_ready"], 1)

            def rstd3(b):
                pool.wait_ge(s["ve3_s"], b + 1)
                g.tensor_tensor(rs3[:, CH * b:CH * b + CH], ve3[:, CH * b:CH * b + CH], mhalf[:, 0:CH], ALU.pow).then_inc(s["rs3_s"], 1)

            def scatter(n):
                c, k = n // TOPK, n % TOPK
                pool.wait_ge(s["xm_ready"], c + 1)
                if n == 0:
                    pool.wait_ge(s["slots_ready"], 1)
                    pool.wait_ge(s["slots_cleared"], 16)
                    pool.wait_ge(s["rows_meta"], 2)
                g.indirect_dma_start(slots_dram, bass.IndirectOffsetOnAxis(ap=slot[:, n:n + 1].bitcast(mybir.dt.uint32), axis=0),
                                     xrow[:, c, k, :], None).then_inc(s["scattered"], 16)

            pool.wait_ge(s["consts"], 1)
            for b in range(3):
                rstd1(b)
            sent = 0
            for b in range(B + 3):
                if b < B:
                    mask(b, 0)
                    mask(b, 1)
                if 2 <= b < B + 2:
                    gated(b - 2)
                if 3 <= b < 3 + TM // S:
                    rstd3(b - 3)
                if b < B:
                    mask(b, 2)
                if 1 <= b <= B:
                    rstd2(b - 1)
                if b + 3 < B:
                    rstd1(b + 3)
                if b < B:
                    mask(b, 3)
                while sent < min(2 * TOPK * max(b - 3, 0), MC * TOPK, 3 * max(b - 3, 0)):
                    scatter(sent)
                    sent += 1
            while sent < MC * TOPK:
                scatter(sent)
                sent += 1
            assert sent == MC * TOPK

            def scatter_y(i, q):
                pool.wait_ge(s["yw_ready"], i + 1)
                number = xb[:, i, D:D + 1]
                g.indirect_dma_start(y_dram, bass.IndirectOffsetOnAxis(ap=number.bitcast(mybir.dt.uint32), axis=0),
                                     yw[q][:, :], None, bounds_check=NA - 1, oob_is_err=False).then_inc(y_out[q], 16)

            for i in range(NB):
                scatter_y(i, i % 2)

        @block.scalar
        def _(act):
            a = nc.scalar
            a.preload_act_table(ACT.Silu)
            act.wait_ge(s["tr_ps"], 1)
            act.wait_ge(s["tab0"], 1)
            for r in range(3):
                a.activation(tabT[:, 0, 32 * r:32 * r + NEST], XB[:, 0:NEST], ACT.Copy)
                a.activation(tabT[:, 1, 32 * r + 16:32 * r + 16 + SEG], XB[:, 16:16 + SEG], ACT.Copy)
            a.activation(cols6[:, :], XB[:, 24:30], ACT.Copy)
            a.activation(posT[:, :, :], XB[:, 256:512].rearrange("p (c n) -> p c n", c=CH), ACT.Copy).then_inc(s["tabs_ready"], 1)
            act.wait_ge(s["pw_ps"], 1)
            a.activation(raw[:, 0, :], XB[:, 256:256 + D], ACT.Copy).then_inc(s["raw_ready"], 1)
            a.activation(PW[:, :, :], XB[:, 0:256].rearrange("p (c n) -> p c n", c=CH), ACT.Copy).then_inc(s["pw_ready"], 1)
            act.wait_ge(s["w1t_ps"], 1)
            a.activation(W1T[:, :, :], PROJ[:, :].rearrange("p (k n) -> p k n", k=4), ACT.Copy).then_inc(s["w1t_ready"], 1)
            a.activation(W2T[:, :], OUTC[:, 0:D], ACT.Copy).then_inc(s["w1t_ready"], 1)
            act.wait_ge(s["tabs_ready"], 1)
            act.wait_ge(s["vz"], 1)

            def evac_x(b):
                act.wait_ge(s["xt_ps"], b + 1)
                if b >= 2:
                    act.wait_ge(s["gv_ps"], b - 1)
                a.activation(xT[:, b % 2, :], XB[:, S:2 * S], ACT.Copy).then_inc(s["xt_ready"], 1)

            def project(b):
                q = b % 2
                act.wait_ge(s["qk_ps"], b + 1)
                if b >= 2:
                    act.wait_ge(s["p3_s"], b - 1)
                for side in range(2):
                    a.activation(qk[:, q, side, :], PROJ[:, side * S:side * S + S], ACT.Silu,
                                 bias=b1_cols[:, 1 + side:2 + side]).then_inc(s["qk_ready"], 1)

            def gate_v(b):
                q = b % R
                act.wait_ge(s["gv_ps"], b + 1)
                if b >= R:
                    act.wait_ge(s["av_done"], 2 * (b - R + 1))
                    act.wait_ge(s["z_ready"], b - R + 1)
                a.activation(gate[:, b % 4, :], PROJ[:, 0:S], ACT.Silu, bias=b1_cols[:, 0:1]).then_inc(s["g_ready"], 1)
                src = PROJ[:, S:2 * S].rearrange("p (c j e r) -> p c j e r", c=CH, e=2, r=HD)
                for e in range(2):
                    a.activation(vpad[:, q, :, e::2, HD * e:HD * e + HD], src[:, :, :, e, :], ACT.Silu).then_inc(s["v_ready"], 1)

            def silu(b, n):
                G = 4 * b + n
                act.wait_ge(s["scores_ps"], G + 1)
                if G >= PR:
                    act.wait_ge(s["av_done"], (G - PR) // 2 + 1)
                i = 2 * (G % 2)
                for k in range(2):
                    last = a.activation(probs[:, G % PR, k, :], bank[SCORE[i + k]][:, 0:SC], ACT.Silu, scale=HD ** -0.5)
                last.then_inc(s["probs_ready"], 1)

            def evac_o(b):
                act.wait_ge(s["av_done"], 2 * b + 2)
                if b:
                    act.wait_ge(s["o_ps"], b)
                a.activation(oT[:, :], OTB[:, 0:S], ACT.Copy).then_inc(s["ot_ready"], 1)

            def affine(b):
                act.wait_ge(s["xot_ps"], b + 1)
                if b:
                    act.wait_ge(s["z_ready"], b)
                a.activation(xa[:, :], OUTC[:, S:2 * S], ACT.Identity, scale=g_col, bias=b_col).then_inc(s["xa_ready"], 1)

            for b in range(2):
                evac_x(b)
                project(b)
                gate_v(b)
            for b in range(B + 3):
                if b < B:
                    silu(b, 0)
                    silu(b, 1)
                if b + 2 < B:
                    evac_x(b + 2)
                if 1 <= b <= B:
                    evac_o(b - 1)
                if b < B:
                    silu(b, 2)
                if 2 <= b < B + 2:
                    affine(b - 2)
                if b + 2 < B:
                    project(b + 2)
                if b < B:
                    silu(b, 3)
                if b + 2 < B:
                    gate_v(b + 2)

            def gelu(i, q, first):
                act.wait_ge(s["hid_ps"], i + 1)
                if not first:
                    act.wait_ge(s["ye_ps"], i - 1)
                a.activation(hid[q][:, :], bank[q][:, :], ACT.Gelu).then_inc(s["hid_ready"], 1)

            gelu(0, 0, True)
            gelu(1, 1, True)
            with act.Fori(2, NB - 2, 2) as i:
                gelu(i, 0, False)
                gelu(i + 1, 1, False)
            if NB % 2:
                gelu(NB - 1, (NB - 1) % 2, False)

        @block.vector
        def _(dve):
            v = nc.vector
            v.memset(mhalf[:, :], -0.5).then_inc(s["consts"], 1)
            v.memset(tabT[:, :, :], 0.0).then_inc(s["tab0"], 1)
            v.memset(raw[:, 1:3, :], 0.0).then_inc(s["raw0"], 1)
            v.memset(ones_bf[:, :], 1.0)
            v.memset(zeros8[:, :], 0.0)
            v.memset(zeroB[:, :], 0.0).then_inc(s["consts"], 1)
            dve.wait_ge(s["ids_in"], 16)
            opens, closes = (40, 91, 123), (41, 93, 125)
            v.tensor_scalar(cmpf[:, 6, :], ids[:, :], 39990.0, None, ALU.is_gt).then_inc(s["sgf"], 1)
            for n in range(3):
                for sign, codes, done in ((0, opens, "o_cnt"), (3, closes, "c_cnt")):
                    if n == 0:
                        v.tensor_scalar(cmpf[:, sign, :], ids[:, :], float(codes[0]), None, ALU.is_equal).then_inc(s[done], 1)
                    else:
                        dve.wait_ge(s[done], n)
                        v.scalar_tensor_tensor(cmpf[:, sign + n, :], ids[:, :], float(codes[n]), cmpf[:, sign + n - 1, :],
                                               ALU.is_equal, ALU.add).then_inc(s[done], 1)
                if n == 0:
                    dve.wait_ge(s["consts"], 2)
                    dve.wait_ge(s["sgf"], 1)
                    v.tensor_tensor_scan(segf[:, :], cmpf[:, 6, :], zeroB[:, :], 0.0, ALU.add, ALU.add).then_inc(s["sgi"], 1)
            dve.wait_ge(s["o_cnt"], 3)
            dve.wait_ge(s["c_cnt"], 3)
            v.tensor_tensor(delta[:, :], cmpf[:, 2, :], cmpf[:, 5, :], ALU.subtract).then_inc(s["del"], 1)
            dve.wait_ge(s["sgi"], 1)
            v.tensor_copy(segi[:, :], segf[:, :]).then_inc(s["sgi"], 1)
            dve.wait_ge(s["del"], 1)
            v.tensor_tensor_scan(depth[:, :], delta[:, :], zeroB[:, :], 0.0, ALU.add, ALU.add).then_inc(s["dep"], 1)
            dve.wait_ge(s["sgi"], 2)
            v.tensor_scalar(segi8[:, :], segi[:, :], 7, None, ALU.bitwise_and).then_inc(s["sgi"], 1)
            dve.wait_ge(s["dep"], 1)
            v.tensor_tensor_scan(lowest[:, :], depth[:, :], zeroB[:, :], 0.0, ALU.min, ALU.min).then_inc(s["low"], 1)
            dve.wait_ge(s["low"], 1)
            v.tensor_tensor(nestf[:, :], depth[:, :], lowest[:, :], ALU.subtract).then_inc(s["nst"], 1)
            dve.wait_ge(s["nst"], 1)
            v.tensor_scalar(code[:, 0, :], nestf[:, :], 0.0, float(NEST - 1), ALU.max, ALU.min).then_inc(s["code_ready"], 1)
            dve.wait_ge(s["sgi"], 3)
            v.tensor_copy(code[:, 1, :], segi8[:, :]).then_inc(s["code_ready"], 1)
            dve.wait_ge(s["rows"], 1)
            v.tensor_scalar(row32[:, :], rowi[:, :], 31, None, ALU.bitwise_and).then_inc(s["idx_ready"], 1)
            dve.wait_ge(s["idx_ready"], 1)
            v.tensor_copy(rowf[:, :], row32[:, :]).then_inc(s["idx_ready"], 1)
            dve.wait_ge(s["idx_ready"], 2)
            v.tensor_scalar(rowge[:, :], rowf[:, :], 16.0, -16.0, ALU.is_ge, ALU.mult).then_inc(s["idx_ready"], 1)
            dve.wait_ge(s["idx_ready"], 3)
            v.tensor_tensor(rowcode[:, :], rowf[:, :], rowge[:, :], ALU.add).then_inc(s["idx_ready"], 1)
            dve.wait_ge(s["raw_ready"], 1)
            dve.wait_ge(s["bias_in"], 96)
            v.tensor_copy(rhs_pieces[:, :, :], raw[:, :, :]).then_inc(s["pc1"], 1)
            dve.wait_ge(s["pc1"], 1)
            v.tensor_tensor(rest[:, :, :], raw[:, :, :], rhs_pieces[:, :, :], ALU.subtract).then_inc(s["pc2"], 1)
            dve.wait_ge(s["pc2"], 1)
            v.tensor_copy(rhs_pieces[32:64, :, :], rest[32:64, :, :])
            v.tensor_copy(piece2[64:96, :, :], rest[64:96, :, :]).then_inc(s["pc3"], 1)
            dve.wait_ge(s["pc3"], 1)
            v.tensor_tensor(rhs_pieces[64:96, :, :], rest[64:96, :, :], piece2[64:96, :, :], ALU.subtract)
            v.memset(rhs_pieces[96:128, :, :], 0.0).then_inc(s["pieces_ready"], 1)
            dve.wait_ge(s["idx_ready"], 4)
            def spread(n):
                dve.wait_ge(s["code_ps"], n + 1)
                v.tensor_scalar(onehot[:, 2 * n:2 * n + 2, :], bank[SCORE[n]][:, :].rearrange("p (b s) -> p b s", b=2),
                                rowcode[:, 0:1], None, ALU.is_equal).then_inc(s["onehot_ready"], 1)

            spread(0)
            dve.wait_ge(s["pw_ready"], 1)

            def embed(b):
                q = b % 2
                hb = h_all[:, CH * b:CH * b + CH, :]
                dve.wait_ge(s["embed_ps"], b + 1)
                v.tensor_tensor(hb, XB[:, 0:S].rearrange("p (c n) -> p c n", c=CH), PW[:, :, :], ALU.add).then_inc(s["h_ready"], 1)
                dve.wait_ge(s["h_ready"], b + 1)
                for c in range(CH):
                    v.bn_stats(bst[:, q, c, :], h_all[:, CH * b + c, :]).then_inc(s["st1"], 1)
                for c in range(CH):
                    dve.wait_ge(s["st1"], CH * b + c + 1)
                    v.bn_aggr(mv1[:, q, c, :], bst[:, q, c, :]).then_inc(s["mv1_s"], 1)
                dve.wait_ge(s["mv1_s"], CH * (b + 1))
                v.tensor_scalar(ve1[:, q, :], mv1[:, q, :, 1], EPS, None, ALU.add).then_inc(s["ve1_s"], 1)

            def normalise(b):
                q = b % 2
                dve.wait_ge(s["rs1_s"], b + 1)
                if b >= 2:
                    dve.wait_ge(s["xt_ps"], b - 1)
                for c in range(CH):
                    v.tensor_scalar(xn[:, q, c, :], h_all[:, CH * b + c, :], mv1[:, q, c, 0:1], rs1[:, q, c:c + 1],
                                    ALU.subtract, ALU.mult).then_inc(s["xn_ready"], 1)

            def split(b):
                q = b % 2
                dve.wait_ge(s["qk_ready"], 2 * (b + 1))
                if b >= 2:
                    for done in bounced:
                        dve.wait_ge(done, 16 * (b - 1))
                v.tensor_copy(qkp[0][:, q, :, :], qk[:, q, :, :]).then_inc(s["p1_s"], 1)
                dve.wait_ge(s["p1_s"], b + 1)
                v.tensor_tensor(qkr[:, q, :, :], qk[:, q, :, :], qkp[0][:, q, :, :], ALU.subtract).then_inc(s["r1_s"], 1)
                dve.wait_ge(s["r1_s"], b + 1)
                v.tensor_copy(qkp[1][:, q, :, :], qkr[:, q, :, :]).then_inc(s["p2_s"], 1)
                dve.wait_ge(s["p2_s"], b + 1)
                v.tensor_tensor(qkp[2][:, q, :, :], qkr[:, q, :, :], qkp[1][:, q, :, :], ALU.subtract).then_inc(s["p3_s"], 1)

            def stats2(b):
                dve.wait_ge(s["o_ps"], b + 1)
                for c in range(CH):
                    v.bn_stats(bst2[:, c, :], OUTC[:, P * c:P * c + P]).then_inc(s["st2"], 1)
                for c in range(CH):
                    dve.wait_ge(s["st2"], CH * b + c + 1)
                    v.bn_aggr(mv2[:, c, :], bst2[:, c, :]).then_inc(s["mv2_s"], 1)
                dve.wait_ge(s["mv2_s"], CH * (b + 1))
                v.tensor_scalar(ve2[:, :], mv2[:, :, 1], EPS, None, ALU.add).then_inc(s["ve2_s"], 1)

            def normalise2(b):
                dve.wait_ge(s["rs2_s"], b + 1)
                if b:
                    dve.wait_ge(s["xot_ps"], b)
                for c in range(CH):
                    v.tensor_scalar(xo[:, c, :], OUTC[:, P * c:P * c + P], mv2[:, c, 0:1], rs2[:, c:c + 1],
                                    ALU.subtract, ALU.mult).then_inc(s["xo_ready"], 1)

            def residual(b):
                hb = h_all[:, CH * b:CH * b + CH, :]
                dve.wait_ge(s["y_ps"], b + 1)
                v.tensor_tensor(hb, PROJ[:, 0:S].rearrange("p (c n) -> p c n", c=CH), hb, ALU.add).then_inc(s["h2_ready"], 1)

            def stats3(b):
                dve.wait_ge(s["h2_ready"], b + 1)
                for c in range(CH * b, CH * b + CH):
                    v.bn_stats(bst3[:, c, :], h_all[:, c, :]).then_inc(s["st3"], 1)
                for c in range(CH * b, CH * b + CH):
                    dve.wait_ge(s["st3"], c + 1)
                    v.bn_aggr(mv3[:, c, :], bst3[:, c, :]).then_inc(s["mv3_s"], 1)
                dve.wait_ge(s["mv3_s"], CH * (b + 1))
                v.tensor_scalar(ve3[:, CH * b:CH * b + CH], mv3[:, CH * b:CH * b + CH, 1], EPS, None, ALU.add).then_inc(s["ve3_s"], 1)

            def normalise3(b):
                dve.wait_ge(s["rs3_s"], b + 1)
                for c in range(CH * b, CH * b + CH):
                    for k in range(TOPK):
                        last = v.tensor_scalar(xrow[:, c, k, 0:D], h_all[:, c, :], mv3[:, c, 0:1], rs3[:, c:c + 1],
                                               ALU.subtract, ALU.mult)
                    last.then_inc(s["xm_ready"], 1)

            def route():
                NJ = MC * TOPK
                dve.wait_ge(s["rts_in"], 32)
                v.tensor_copy(re_f[:, :], re_i[:, :, :].rearrange("p c k -> p (c k)")).then_inc(s["e_f"], 1)
                v.memset(restart[:, :, :], 1.0).then_inc(s["restart_s"], 1)
                dve.wait_ge(s["e_f"], 1)
                for e in range(E):
                    last = v.tensor_scalar(chosen[:, e, :], re_f[:, :], float(e), None, ALU.is_equal)
                last.then_inc(s["chosen_s"], 1)
                dve.wait_ge(s["restart_s"], 1)
                v.memset(restart[:, :, 0:1], 0.0).then_inc(s["restart_s"], 1)
                dve.wait_ge(s["restart_s"], 2)
                dve.wait_ge(s["chosen_s"], 1)
                v.tensor_tensor_scan(rank[:, :, :].rearrange("p e j -> p (e j)"), restart[:, :, :].rearrange("p e j -> p (e j)"),
                                     chosen[:, :, :].rearrange("p e j -> p (e j)"), 0.0, ALU.mult, ALU.add).then_inc(s["ranked"], 1)
                dve.wait_ge(s["ranked"], 1)
                v.tensor_copy(count_bf[:, :], rank[:, :, NJ - 1]).then_inc(s["counted"], 1)
                dve.wait_ge(s["prefix_ps"], 1)
                v.tensor_copy(prefix[:, :, :], bank[3][:, 0:2 * E].rearrange("p (a e) -> p a e", a=2)).then_inc(s["prefix_ready"], 1)
                dve.wait_ge(s["prefix_ready"], 1)
                steps = 0

                def then(ins):
                    nonlocal steps
                    steps += 1
                    ins.then_inc(s["rnd"], 1)
                    dve.wait_ge(s["rnd"], steps)

                then(v.tensor_scalar(full_i[:, :], prefix[:, 1, :], float(P - 1), None, ALU.add))
                then(v.tensor_scalar(blocks_i[:, :], full_i[:, :], P.bit_length() - 1, None, ALU.arith_shift_right))
                then(v.tensor_copy(blocks[:, :], blocks_i[:, :]))
                then(v.tensor_tensor_scan(ends[:, :], blocks[:, :], zeros8[:, :], 0.0, ALU.add, ALU.add))
                then(v.tensor_tensor(starts[:, :], ends[:, :], blocks[:, :], ALU.subtract))
                then(v.scalar_tensor_tensor(offset[:, :], starts[:, :], float(P), prefix[:, 0, :], ALU.mult, ALU.add))
                then(v.tensor_tensor(place[:, :, :], rank[:, :, :], offset[:, :].unsqueeze(2).to_broadcast([P, E, NJ]), ALU.add))
                then(v.tensor_tensor(placed[:, :, :], place[:, :, :], chosen[:, :, :], ALU.mult))
                then(v.tensor_reduce(slot_f[:, :], placed[:, :, :].rearrange("p e j -> p j e"), mybir.AxisListType.X, ALU.add))
                v.tensor_scalar(slot[:, :], slot_f[:, :], -1.0, None, ALU.add).then_inc(s["slots_ready"], 1)
                dve.wait_ge(s["rows"], 2)
                then(v.tensor_tensor(passed[:, :, :], block_no[:, :, :], ends[:, :].unsqueeze(1).to_broadcast([P, NB, E]), ALU.is_ge))
                then(v.tensor_reduce(owner_f[:, :], passed[:, :, :], mybir.AxisListType.X, ALU.add))
                v.tensor_scalar(owner[:, :], owner_f[:, :], float(E - 1), None, ALU.min).then_inc(s["owner_ready"], 1)

            embed(0)
            for n in range(1, B // 2):
                spread(n)
            normalise(0)
            embed(1)
            split(0)
            normalise(1)
            embed(2)
            split(1)
            route()
            for b in range(B + 3):
                if b + 2 < B:
                    normalise(b + 2)
                if 2 <= b < B + 2:
                    normalise2(b - 2)
                if b >= 3:
                    residual(b - 3)
                if 3 <= b < 3 + TM // S:
                    stats3(b - 3)
                if 1 <= b <= B:
                    stats2(b - 1)
                if b + 3 < B:
                    embed(b + 3)
                if 3 <= b < 3 + TM // S:
                    normalise3(b - 3)
                if b + 2 < B:
                    split(b + 2)

            for n in range(0, NB, 4):
                m = min(4, NB - n)
                dve.wait_ge(s["xbt_ps"], n // 4 + 1)
                v.tensor_copy(xbT[:, P * n:P * (n + m)], bank[4 + (n // 4) % 2][:, 0:P * m]).then_inc(s["xbt_ready"], 1)

            def weigh(i, q, first):
                dve.wait_ge(s["ye_ps"], i + 1)
                if not first:
                    dve.wait_ge(y_out[q], (i - q) * 8)
                v.tensor_scalar(yw[q][:, :], bank[6 + q][:, 0:D], xb[:, bass.ds(i, 1), D + 1], None, ALU.mult).then_inc(s["yw_ready"], 1)

            weigh(0, 0, True)
            weigh(1, 1, True)
            with dve.Fori(2, NB - 2, 2) as i:
                weigh(i, 0, False)
                weigh(i + 1, 1, False)
            weigh(NB - 1, 0, False)
            for n in range(0, MC, 2):
                dve.wait_ge(s["yb_in"], 16 * (n // 2 + 1))
                v.tensor_tensor(ysum[:, n:n + 2, :], yb[:, n:n + 2, 0, :], yb[:, n:n + 2, 1, :], ALU.add).then_inc(s["ysum_ready"], 1)
            for n in range(0, MC, 2):
                dve.wait_ge(s["ysum_ready"], n // 2 + 1)
                v.tensor_tensor(ysum[:, n:n + 2, :], ysum[:, n:n + 2, :], h_all[:, n:n + 2, :], ALU.add).then_inc(s["out_ready"], 1)

        @block.tensor
        def _(pe):
            mm = nc.tensor.matmul
            tr = nc.tensor.transpose
            pe.wait_ge(s["ident_ready"], 1)
            pe.wait_ge(s["small_in"], 48)
            pe.wait_ge(s["pos_in"], 16)
            tr(XB[:, 0:NEST], nest_sb[:, :], ident[0:NEST, 0:NEST])
            tr(XB[:, 16:16 + SEG], seg_sb[:, :], ident[0:SEG, 0:SEG])
            pe.wait_ge(s["cols_in"], 48)
            tr(XB[:, 24:30], rows6[:, :], ident[0:6, 0:6])
            for c in range(CH):
                last = tr(XB[:, 256 + P * c:256 + P * c + P], pos_sb[:, c, :], ident[:, :])
            last.then_inc(s["tr_ps"], 1)
            pe.wait_ge(s["tabs_ready"], 1)
            for c in range(CH):
                mm(XB[:, P * c:P * c + P], posT[:, c, :], tokW_sb[:, 0, :], start=True, stop=True)
            mm(XB[:, 256:256 + D], tabT[:, 0, :], tokW_sb[:, 1, :], start=True, stop=False)
            mm(XB[:, 256:256 + D], tabT[:, 1, :], tokW_sb[:, 2, :], start=False, stop=True).then_inc(s["pw_ps"], 1)
            pe.wait_ge(s["attnw_in"], 32)
            for k in range(4):
                tr(PROJ[:, P * k:P * k + P], W1_sb[:, k, :], ident[:, :])
            tr(OUTC[:, 0:D], W2_sb[:, :], ident[:, :]).then_inc(s["w1t_ps"], 1)
            pe.wait_ge(s["code_ready"], 2)
            pe.wait_ge(s["sel_ready"], 2)
            for n in range(B // 2):
                for b in (2 * n, 2 * n + 1):
                    dst = bank[SCORE[n]][:, S * (b % 2):S * (b % 2) + S]
                    mm(dst, sel[:, 0, b, :], code[:, 0, :], start=True, stop=False)
                    last = mm(dst, sel[:, 1, b, :], code[:, 1, :], start=False, stop=True)
                last.then_inc(s["code_ps"], 1)

            def embed(b):
                pe.wait_ge(s["onehot_ready"], b // 2 + 1)
                if b == 0:
                    pe.wait_ge(s["pieces_ready"], 1)
                if b >= 1:
                    pe.wait_ge(s["xt_ready"], b)
                    pe.wait_ge(s["h_ready"], b)
                for c in range(CH):
                    last = mm(XB[:, P * c:P * c + P], onehot[:, b, P * c:P * c + P], rhs_pieces[:, 0, :], start=True, stop=True)
                last.then_inc(s["embed_ps"], 1)

            def transpose_x(b):
                pe.wait_ge(s["xn_ready"], CH * (b + 1))
                pe.wait_ge(s["h_ready"], b + 1)
                for c in range(CH):
                    last = tr(XB[:, S + P * c:S + P * c + P], xn[:, b % 2, c, :], ident[:, :])
                last.then_inc(s["xt_ps"], 1)

            def project_qk(b):
                pe.wait_ge(s["xt_ready"], b + 1)
                if b == 0:
                    pe.wait_ge(s["w1t_ready"], 2)
                if b:
                    pe.wait_ge(s["v_ready"], 2 * b)
                if b >= 5:
                    pe.wait_ge(s["h2_ready"], b - 4)
                for side in range(2):
                    last = mm(PROJ[:, side * S:side * S + S], W1T[:, 1 + side, :], xT[:, b % 2, :], start=True, stop=True)
                last.then_inc(s["qk_ps"], 1)

            def project_gv(b):
                pe.wait_ge(s["qk_ready"], 2 * (b + 1))
                mm(PROJ[:, 0:S], W1T[:, 0, :], xT[:, b % 2, :], start=True, stop=True)
                for c in range(CH):
                    dst = PROJ[:, S + P * c:S + P * c + P]
                    mm(dst, xT[:, b % 2, P * c:P * c + P], W1T[:, 3, :], start=True, stop=False)
                    last = mm(dst, ones_bf[:, :], rhs_pieces[:, 1, :], start=False, stop=True)
                last.then_inc(s["gv_ps"], 1)

            def scores(b, n):
                G, q = 4 * b + n, b % R
                if n == 0:
                    pe.wait_ge(stk[q], 16 * NDMA * (b // R + 1))
                if G >= 2:
                    pe.wait_ge(s["probs_ready"], G - 1)
                i = 2 * (G % 2)
                for k, h in enumerate(HALVES[n // 2][2 * (n % 2):2 * (n % 2) + 2]):
                    dst, kk, qq = bank[SCORE[i + k]], stacks[:, q, 1, h, :], stacks[:, q, 0, h, :]
                    mm(dst[:, P:SC], kk[:, 0:P], qq, start=True, stop=True)
                    last = mm(dst[:, 0:P], kk[:, P:S], qq[:, P:S], start=True, stop=True)
                last.then_inc(s["scores_ps"], 1)

            def attend(b, half):
                q = b % R
                pe.wait_ge(s["masked"], 4 * b + 2 * half + 2)
                if half == 0:
                    pe.wait_ge(s["v_ready"], 2 * (b + 1))
                    if b:
                        pe.wait_ge(s["ot_ready"], b)
                for c in range(CH):
                    for j, h in enumerate(HALVES[half]):
                        pr = probs[:, (4 * b + 2 * half + j // 2) % PR, j % 2, :]
                        dst = OTB[32 * j:32 * j + 32, P * c:S]
                        last = mm(dst, vpad[:, q, c, h, :], pr[:, P:SC] if c == 0 else pr[:, 0:P],
                                  start=(half == 0 and c == 0), stop=(half == 1 and c == 1), skip_group_check=True)
                last.then_inc(s["av_done"], 1)

            def transpose_o(b):
                pe.wait_ge(s["ot_ready"], b + 1)
                if b:
                    pe.wait_ge(s["xa_ready"], b)
                for c in range(CH):
                    last = tr(OUTC[:, P * c:P * c + P], oT[:, P * c:P * c + P], ident[:, :])
                last.then_inc(s["o_ps"], 1)

            def transpose_xo(b):
                pe.wait_ge(s["xo_ready"], CH * (b + 1))
                for c in range(CH):
                    last = tr(OUTC[:, S + P * c:S + P * c + P], xo[:, c, :], ident[:, :])
                last.then_inc(s["xot_ps"], 1)

            def out_proj(b):
                pe.wait_ge(s["z_ready"], b + 1)
                pe.wait_ge(s["v_ready"], 2 * min(b + 5, B))
                if b:
                    pe.wait_ge(s["h2_ready"], b)
                for c in range(CH):
                    dst = PROJ[:, P * c:P * c + P]
                    mm(dst, z[:, P * c:P * c + P], W2T[:, :], start=True, stop=False)
                    last = mm(dst, ones_bf[:, :], rhs_pieces[:, 2, :], start=False, stop=True)
                last.then_inc(s["y_ps"], 1)

            pe.wait_ge(s["pw_ready"], 1)
            embed(0)
            transpose_x(0)
            embed(1)
            project_qk(0)
            project_gv(0)
            transpose_x(1)
            embed(2)
            project_qk(1)
            project_gv(1)
            pe.wait_ge(s["onehot_ready"], 4)
            pe.wait_ge(s["upper_ready"], 1)
            pe.wait_ge(s["counted"], 1)
            mm(bank[3][:, 0:E], upper[:, :], count_bf[:, :], start=True, stop=True)
            mm(bank[3][:, E:2 * E], ones_bf[:, :], count_bf[:, :], start=True, stop=True).then_inc(s["prefix_ps"], 1)
            for b in range(B + 3):
                if b < B:
                    scores(b, 0)
                    if b == 0:
                        pe.wait_ge(s["prefix_ready"], 1)
                    scores(b, 1)
                if 1 <= b <= B:
                    attend(b - 1, 1)
                if b + 2 < B:
                    transpose_x(b + 2)
                if b >= 3:
                    out_proj(b - 3)
                if 2 <= b < B + 2:
                    transpose_xo(b - 2)
                if b < B:
                    scores(b, 2)
                if 1 <= b <= B:
                    transpose_o(b - 1)
                if b + 2 < B:
                    project_qk(b + 2)
                if b + 3 < B:
                    embed(b + 3)
                if b < B:
                    scores(b, 3)
                if b + 2 < B:
                    project_gv(b + 2)
                if b < B:
                    attend(b, 0)

            for n in range(0, NB, 4):
                m = min(4, NB - n)
                pe.wait_ge(s["xb_in"], 16 * (n // 4 + 1))
                if n >= 8:
                    pe.wait_ge(s["xbt_ready"], n // 4 - 1)
                else:
                    pe.wait_ge(s["h2_ready"], B)
                for i in range(m):
                    last = tr(bank[4 + (n // 4) % 2][:, P * i:P * i + P], xb[:, n + i, 0:D], ident[:, :])
                last.then_inc(s["xbt_ps"], 1)
            pe.wait_ge(s["w2_in"], 16)
            pe.wait_ge(s["owner_ready"], 1)
            pe.wait_ge(s["xbt_ready"], (NB + 3) // 4)

            def up(i, q, first):
                pe.wait_ge(w1_in[q], 16 * (i // 2 + 1) if isinstance(i, int) else (i + 2 - q) * 8)
                if not first:
                    pe.wait_ge(s["hid_ready"], i - 1)
                for f in range(FC):
                    last = mm(bank[q][:, P * f:P * f + P], w1s[q][:, P * f:P * f + P], xbT[:, bass.ds(i * P, P)], start=True, stop=True)
                last.then_inc(s["hid_ps"], 1)

            def down(i, q, first):
                pe.wait_ge(s["hid_ready"], i + 1)
                if not first:
                    pe.wait_ge(s["yw_ready"], i - 1)
                e = pe.value_load(owner[0:1, bass.ds(i, 1)], min_val=0, max_val=E - 1)
                for f in range(FC):
                    last = mm(bank[6 + q][:, 0:D], hid[q][:, P * f:P * f + P], w2_sb[:, bass.ds(e * (FC * D) + f * D, D)],
                              start=(f == 0), stop=(f == FC - 1))
                last.then_inc(s["ye_ps"], 1)

            up(0, 0, True)
            up(1, 1, True)
            down(0, 0, True)
            up(2, 0, False)
            down(1, 1, True)
            with pe.Fori(2, NB - 2, 2) as i:
                up(i + 1, 1, False)
                down(i, 0, False)
                up(i + 2, 0, False)
                down(i + 1, 1, False)
            assert NB % 2
            down(NB - 1, 0, False)


_INS = ["x", "L0_tok_pos_table", "L0_tok_nest_table", "L0_tok_seg_table", "L0_tok_W", "L0_attn_W1", "L0_attn_b1",
        "L0_attn_ln_g", "L0_attn_ln_b", "L0_attn_W2", "L0_attn_b2", "L0_ffn_expert_weights", "L0_ffn_expert_indices",
        "L0_ffn_w1", "L0_ffn_w2"]


def kernel(**inputs):
    import numpy as np
    import concourse.bacc as bacc
    from concourse import mybir
    from concourse.bass_utils import run_bass_kernel_spmd

    nc = bacc.Bacc("TRN2", target_bir_lowering=False, num_devices=1)
    arrays, args = {}, []
    for name in _INS:
        a = np.ascontiguousarray(inputs[name])
        arrays[f"in_{name}"] = a
        args.append(nc.dram_tensor(f"in_{name}", a.shape, mybir.dt.from_np(a.dtype), kind="ExternalInput").ap())
    out = nc.dram_tensor("out", (8, 256, 128), mybir.dt.float32, kind="ExternalOutput").ap()
    build(nc, *args, out)
    r = run_bass_kernel_spmd(nc, [arrays], core_ids=[0])
    return r.results[0]["out"]
```

```python
import concourse.bass as bass
from concourse import mybir
from contextlib import ExitStack

F32, BF16, I32 = mybir.dt.float32, mybir.dt.bfloat16, mybir.dt.int32
ALU = mybir.AluOpType
ACT = mybir.ActivationFunctionType

P = 128
B, S, D = 8, 256, 128
CH = S // P
NC = B * CH
H, HD = 8, 16
NEST, SEG = 16, 8
PIECES = ((0, 0), (0, 1), (1, 0), (0, 2), (1, 1), (2, 0))
KS = HD * len(PIECES)
SC = S + P
HALVES = ((0, 2, 4, 6), (1, 3, 5, 7))
E, FF = 8, 512
FC = FF // P
TM = 1024
MC = TM // P
TOPK = 2
NA = TM * TOPK
NB = (NA + E * (P - 1)) // P
ROW = D + 2
NOBODY = 1 << 20
EPS = 1e-5
PR = 8
RING = 4
LOOPED = NB // RING * RING
AHEAD = 4
R = AHEAD
QUOTAS = {4: (1, 1, 2), 5: (1, 1, 2), 6: (1, 1, 2), 7: (1, 2, 1)}
GR = AHEAD + 2
LATE = B - AHEAD - 1


def build(nc, x, pos_table, nest_table, seg_table, tok_W, W1, b1, ln_g, ln_b, W2, b2, route_w, route_e, w1, w2, out):
    ctx = ExitStack()
    with ctx:
        def sb(name, shape, dt=F32):
            return ctx.enter_context(nc.sbuf_tensor(name, shape, dt))

        def pb(name):
            return ctx.enter_context(nc.psum_tensor(name, [P, 512], F32))

        def sem(name):
            return ctx.enter_context(nc.semaphore(name))

        ident = sb("ident", [P, P])
        ids = sb("ids", [B, S], I32)
        nest_sb = sb("nest_sb", [NEST, D])
        seg_sb = sb("seg_sb", [SEG, D])
        tokW_sb = sb("tokW_sb", [P, 3, D])
        pos_sb = sb("pos_sb", [P, CH, D])
        W1_sb = sb("W1_sb", [P, 4, D])
        W2_sb = sb("W2_sb", [P, D])
        rows6 = sb("rows6", [6, P])
        rows6_rh = sb("rows6_rh", [6, P])
        cols6 = sb("cols6", [P, 2, 6])
        gate_col, q_col, k_col, g_col, b_col = cols6[:, 0, 0:1], cols6[:, 1, 1:2], cols6[:, 1, 2:3], cols6[:, 0, 4:5], cols6[:, 0, 5:6]
        W1T = sb("W1T", [P, 4, P])
        W2T = sb("W2T", [P, D])
        posT = sb("posT", [P, CH, P])
        tabT = sb("tabT", [P, 2, P])
        PW = sb("PW", [P, CH, D])
        raw = sb("raw", [P, 3, D])
        rest = sb("rest", [P, 3, D])
        piece2 = sb("piece2", [P, 3, D], BF16)
        rhs_pieces = sb("rhs_pieces", [P, 3, D], BF16)
        ones_bf = sb("ones_bf", [P, P], BF16)
        delta = sb("delta", [B, S])
        depth = sb("depth", [B, S])
        lowest = sb("lowest", [B, S])
        zeroB = sb("zeroB", [B, S])
        code = sb("code", [B, 2, S], BF16)
        sel = sb("sel", [B, 2, B, P], BF16)
        rowi = sb("rowi", [P, 1], I32)
        row32 = sb("row32", [P, 1], I32)
        rowf = sb("rowf", [P, 1])
        rowge = sb("rowge", [P, 1])
        rowcode = sb("rowcode", [P, 1])
        onehot = sb("onehot", [P, B, S], BF16)
        h_all = sb("h_all", [P, NC, D])
        STAT_X, STAT_O, STAT_H = range(3)
        bst = sb("bst", [P, 2, 3, CH, 6])
        mv = sb("mv", [P, 2, 3, CH, 2])
        ve = sb("ve", [P, 2, 3, CH])
        rstd = sb("rstd", [P, 2, 3, CH])
        mhalf = sb("mhalf", [P, 3, CH])
        xn = sb("xn", [P, 2, CH, D])
        xT = sb("xT", [P, 2, S])
        qk = sb("qk", [P, 2, 2, S])
        qkp = sb("qkp", [P, 2, 2, 3, S], BF16)
        qkr = sb("qkr", [P, 2, 2, S])
        stacks = sb("stacks", [KS, R, H, 2, S], BF16)
        gate = sb("gate", [P, GR, S])
        vpad = sb("vpad", [P, R, CH, H, 32])
        probs = sb("probs", [P, PR, 2, SC])
        oT = sb("oT", [P, S])
        xo = sb("xo", [P, CH, D])
        xa = sb("xa", [P, S])
        z = sb("z", [P, S])
        below = sb("below", [P, P])
        future = sb("future", [P, P], mybir.dt.uint8)
        zeros = sb("zeros", [P, P])
        upper = sb("upper", [P, P], BF16)
        re_i = sb("re_i", [P, MC, TOPK], I32)
        re_f = sb("re_f", [P, MC * TOPK])
        rw = sb("rw", [P, MC, TOPK])
        chosen = sb("chosen", [P, E, MC * TOPK])
        restart = sb("restart", [P, E, MC * TOPK])
        rank = sb("rank", [P, E, MC * TOPK])
        count_bf = sb("count_bf", [P, E], BF16)
        zeros8 = sb("zeros8", [P, E])
        prefix = sb("prefix", [P, 2, E])
        full_i = sb("full_i", [P, E], I32)
        blocks_i = sb("blocks_i", [P, E], I32)
        blocks = sb("blocks", [P, E])
        ends = sb("ends", [P, E])
        starts = sb("starts", [P, E])
        offset = sb("offset", [P, E])
        place = sb("place", [P, E, MC * TOPK])
        placed = sb("placed", [P, E, MC * TOPK])
        slot_f = sb("slot_f", [P, MC * TOPK])
        slot = sb("slot", [P, MC * TOPK], I32)
        block_no = sb("block_no", [P, NB, E])
        passed = sb("passed", [P, NB, E])
        owner_f = sb("owner_f", [P, NB])
        owner = sb("owner", [P, NB], I32)
        xrow = sb("xrow", [P, MC, TOPK, ROW])
        xb = sb("xb", [P, NB, ROW])
        xbT = sb("xbT", [P, NB * P])

        def scan_row(n, dt=F32):
            v = xbT[0:B, S * n:S * (n + 1)]
            return v if dt == F32 else v.bitcast(dt)

        cmpf = xbT[0:B, 0:7 * S].rearrange("b (n s) -> b n s", s=S)
        nestf, segf, segi, segi8 = scan_row(7), scan_row(8), scan_row(9, I32), scan_row(10, I32)
        w1s = [sb(f"w1s{i}", [P, FF]) for i in range(RING)]
        w2_sb = sb("w2_sb", [P, E * FC * D])
        hid = [sb(f"hid{i}", [P, FF]) for i in range(RING)]
        yw = [sb(f"yw{i}", [P, D]) for i in range(RING)]
        spent = probs[:, :, :, :].rearrange("p g a n -> p (g a n)")
        yb = spent[:, 0:NA // P * D].rearrange("p (c k d) -> p c k d", k=TOPK, d=D)
        ysum = spent[:, NA // P * D:NA // P * D + MC * D].rearrange("p (c d) -> p c d", d=D)
        slots_dram = nc.dram_tensor("slots_dram", (NB * P, ROW), F32, kind="Internal").ap()
        y_dram = nc.dram_tensor("y_dram", (NA, D), F32, kind="Internal").ap()

        bank = [pb(f"bank{i}") for i in range(8)]
        SCORE, PROJ, OUTC, OTB, XB = (0, 1, 2, 3), bank[4], bank[5], bank[6], bank[7]

        def x_bank(b):
            return (bank[0], OTB, OUTC, XB)[b] if b < AHEAD else XB

        def o_bank(b):
            return PROJ if b >= AHEAD and b % 2 == 0 else OUTC

        def gv_bank(b):
            return bank[1 + b] if b < AHEAD - 1 else PROJ

        names = """ids_in tables_in bias_rows_in attnw_in bias_pieces_in tokw_in routes_in w2_in ident_zeroed ident_ready sel_filled
        sel_ready upper_filled upper_ready ones_ready constants_ready numbers_ready row_codes opens_found closes_found
        steps_ready depth_ready lowest_ready nest_ready segments_ready segment_marks code_ready tables_zeroed
        rows_reordered tables_ps tabs_ready weights_ps weights_ready products_ps positions_ready raw_zeroed raw_ready
        first_piece_ready rest_ready second_piece_ready pieces_ready code_ps onehot_ready embed_ps h_ready x_stats
        x_moments x_variances x_roots stats moments variances roots xn_ready xt_ps xt_ready qk_ps qk_ready gv_ps
        g_ready v_ready first_pieces remainders second_pieces third_pieces scores_ps probs_ready masked masked_dve
        below_ready future_ready av_done ot_ready o_ps xo_ready xot_ps xa_ready z_ready y_ps h2_ready stored
        values_zeroed experts_read choices_ready restarts_ready ranked counted prefix_ps prefix_ready routing_steps
        slots_ready owner_ready slots_filled slots_cleared numbers_beside_rows rows_ready scattered xbt_ps xbt_ready
        hid_ps hid_ready ye_ps yw_ready ysum_ready out_ready"""
        s = {n: sem(n) for n in names.split()}
        w1_in = [sem(f"w1_in{i}") for i in range(RING)]
        y_out = [sem(f"y_out{i}") for i in range(RING)]
        XB_PARTS = [(n, min(4, NB - n)) for n in range(0, NB, 4)]
        SLOT_BANKS = (4, 2, 4, 3, 4, 5)
        xb_in = [sem(f"xb_in{i}") for i in range(len(XB_PARTS))]
        yb_in = [sem(f"yb_in{i}") for i in range(MC // 2)]
        stk = [sem(f"stacks_in{i}") for i in range(R)]

        def by_pool(b, n):
            return b < LATE + 2 or (b == LATE + 2 and n % 2 == 0)

        def masked_before(b, n):
            pool_groups = sum(by_pool(g // 4, g % 4) for g in range(4 * b + n + 1))
            return pool_groups, 4 * b + n + 1 - pool_groups

        def later_parts(step):
            return [n for n, b, count in ((STAT_O, step - 1, B), (STAT_H, step - 3, TM // S)) if 0 <= b < count]

        block = ctx.enter_context(nc.Block())

        @block.sync
        def _(sp):
            sp.dma_start(ids[:, :], x).then_inc(s["ids_in"], 16)
            sp.dma_start(nest_sb[:, :], nest_table).then_inc(s["tables_in"], 16)
            sp.dma_start(seg_sb[:, :], seg_table).then_inc(s["tables_in"], 16)
            sp.dma_start(pos_sb[:, :, :], pos_table[0:S, :].rearrange("(c p) n -> p c n", p=P)).then_inc(s["tables_in"], 16)
            sp.dma_start(rows6[0:4, :], b1.rearrange("(k p) -> k p", p=P)).then_inc(s["bias_rows_in"], 16)
            sp.dma_start(rows6[4:5, :], ln_g.rearrange("(a p) -> a p", a=1)).then_inc(s["bias_rows_in"], 16)
            sp.dma_start(rows6[5:6, :], ln_b.rearrange("(a p) -> a p", a=1)).then_inc(s["bias_rows_in"], 16)
            sp.dma_start(tokW_sb[:, :, :], tok_W.rearrange("(k p) n -> p k n", p=P)).then_inc(s["tokw_in"], 16)
            sp.wait_ge(s["raw_zeroed"], 1)
            for r in range(3):
                sp.dma_start(raw[32 * r:32 * r + 1, 1, :], b1[3 * P:4 * P].rearrange("(a n) -> a n", a=1)).then_inc(s["bias_pieces_in"], 16)
                sp.dma_start(raw[32 * r:32 * r + 1, 2, :], b2.rearrange("(a n) -> a n", a=1)).then_inc(s["bias_pieces_in"], 16)
            sp.dma_start(W1_sb[:, :, :], W1.rearrange("(k p) n -> p k n", p=P)).then_inc(s["attnw_in"], 16)
            sp.dma_start(W2_sb[:, :], W2).then_inc(s["attnw_in"], 16)
            sp.dma_start(re_i[:, :, :], route_e.rearrange("(c p) k -> p c k", p=P)).then_inc(s["routes_in"], 16)
            sp.dma_start(rw[:, :, :], route_w.rearrange("(c p) k -> p c k", p=P)).then_inc(s["routes_in"], 16)

            def stack(b):
                q = b % 2
                if b >= R:
                    sp.wait_ge(s["scores_ps"], 4 * (b - R + 1))
                pieces = qkp[:, q, :, :, :].rearrange("p a i s -> p (a i) s")
                for slot, (qi, ki) in sorted(enumerate(PIECES), key=lambda x: max(x[1])):
                    sp.wait_ge(s[("first_pieces", "second_pieces", "third_pieces")[max(qi, ki)]], b + 1)
                    pair = pieces[:, qi:3 + ki + 1:3 + ki - qi, :]
                    sp.dma_start(stacks[HD * slot:HD * (slot + 1), b % R, :, :, :], pair).then_inc(stk[b % R], 16)

            def store(b):
                sp.wait_ge(s["h2_ready"], b + 1)
                sp.dma_start(out[b].rearrange("(c p) d -> p c d", p=P), h_all[:, CH * b:CH * b + CH, :]).then_inc(s["stored"], 16)

            sp.wait_ge(s["slots_filled"], 2)
            sp.dma_start(slots_dram.rearrange("(i p) n -> p i n", p=P), xb[:, :, :]).then_inc(s["slots_cleared"], 16)
            for b in range(B):
                stack(b)
                if b >= B // 2:
                    n = E // (B // 2)
                    e = (b - B // 2) * n
                    sp.dma_start(w2_sb[:, FC * D * e:FC * D * (e + n)].rearrange("p (g d) -> p g d", d=D),
                                 w2[e:e + n].rearrange("e (c p) d -> p (e c) d", p=P)).then_inc(s["w2_in"], 16)

            def stage(i, q, first):
                if not first:
                    sp.wait_ge(s["hid_ps"], i - RING + 1)
                e = sp.value_load(owner[0:1, bass.ds(i, 1)], min_val=0, max_val=E - 1)
                sp.dma_start(w1s[q][:, :], w1[bass.ds(e, 1)].rearrange("a p f -> (a p) f")).then_inc(w1_in[q], 16)

            sp.wait_ge(s["owner_ready"], 1)
            for i in range(RING):
                stage(i, i, True)
            for b in range(TM // S, B - 1):
                store(b)
            sp.wait_ge(s["scattered"], 16 * MC * TOPK)
            for j, (n, m) in enumerate(XB_PARTS):
                sp.dma_start(xb[:, n:n + m, :], slots_dram[P * n:P * (n + m), :].rearrange("(i p) n -> p i n", p=P)).then_inc(xb_in[j], 16)
            store(B - 1)
            with sp.Fori(RING, LOOPED, RING) as i:
                for q in range(RING):
                    stage(i + q, q, False)
            for i in range(LOOPED, NB):
                stage(i, i % RING, False)

            for q in range(RING):
                sp.wait_ge(y_out[q], 16 * len(range(q, NB, RING)))
            for j in range(MC // 2):
                n = 2 * j
                sp.dma_start(yb[:, n:n + 2, :, :], y_dram[TOPK * P * n:TOPK * P * (n + 2), :].rearrange("(c p k) d -> p c k d", p=P, k=TOPK)).then_inc(yb_in[j], 16)
            for n in range(0, MC, 2):
                sp.wait_ge(s["out_ready"], n // 2 + 1)
                sp.dma_start(out[n // 2].rearrange("(c p) d -> p c d", p=P), ysum[:, n:n + 2, :]).then_inc(s["stored"], 16)
            sp.wait_ge(s["stored"], 16 * B)

        @block.gpsimd
        def _(pool):
            g = nc.gpsimd
            g.memset(ident[:, :], 0.0).then_inc(s["ident_zeroed"], 1)
            g.memset(sel[:, :, :, :], 0.0).then_inc(s["sel_filled"], 1)
            g.memset(upper[:, :], 1.0).then_inc(s["upper_filled"], 1)
            pool.wait_ge(s["ident_zeroed"], 1)
            g.affine_select(out=ident[:, :], in_=ident[:, :], compare_op=ALU.not_equal, fill=1.0, base=0,
                            pattern=[[-1, P]], channel_multiplier=1).then_inc(s["ident_ready"], 1)
            g.iota(rowi[:, :], pattern=[[0, 1]], base=0, channel_multiplier=1).then_inc(s["numbers_ready"], 1)
            pool.wait_ge(s["sel_filled"], 1)
            v = sel[:, :, :, :].rearrange("k t b (q r) -> k t b q r", r=32)
            for t in range(2):
                for r in range(3):
                    g.memset(v[:, t, :, r, 16 * t:16 * t + (NEST, SEG)[t]], 1.0).then_inc(s["sel_filled"], 1)
            pool.wait_ge(s["sel_filled"], 7)
            for t in range(2):
                g.affine_select(out=sel[:, t, :, :], in_=sel[:, t, :, :], compare_op=ALU.is_equal, fill=0.0, base=0,
                                pattern=[[1, B], [0, P]], channel_multiplier=-1).then_inc(s["sel_ready"], 1)
            g.iota(below[:, :], pattern=[[-1, P]], base=0, channel_multiplier=1, allow_small_or_imprecise_dtypes=True).then_inc(s["below_ready"], 1)
            g.memset(vpad[:, :, :, :, :], 0.0).then_inc(s["values_zeroed"], 1)
            pool.wait_ge(s["upper_filled"], 1)
            g.affine_select(out=upper[:, :], in_=upper[:, :], compare_op=ALU.is_gt, fill=0.0, base=0,
                            pattern=[[1, P]], channel_multiplier=-1).then_inc(s["upper_ready"], 1)
            g.memset(xb[:, :, :], 0.0).then_inc(s["slots_filled"], 1)
            pool.wait_ge(s["slots_filled"], 1)
            g.memset(xb[:, :, D:D + 1].bitcast(I32), NOBODY).then_inc(s["slots_filled"], 1)
            g.iota(block_no[:, :, :], pattern=[[1, NB], [0, E]], base=0, channel_multiplier=0, allow_small_or_imprecise_dtypes=True).then_inc(s["numbers_ready"], 1)
            g.iota(xrow[:, :, :, D:D + 1].bitcast(I32), pattern=[[TOPK * P, MC], [1, TOPK], [0, 1]], base=0, channel_multiplier=TOPK).then_inc(s["numbers_beside_rows"], 1)
            pool.wait_ge(s["routes_in"], 32)
            g.tensor_copy(xrow[:, :, :, D + 1:D + 2], rw[:, :, :]).then_inc(s["numbers_beside_rows"], 1)

            def root_x(b):
                pool.wait_ge(s["x_variances"], b + 1)
                g.tensor_tensor(rstd[:, b % 2, STAT_X, :], ve[:, b % 2, STAT_X, :], mhalf[:, STAT_X, :], ALU.pow).then_inc(s["x_roots"], 1)

            def root(step):
                pool.wait_ge(s["variances"], step)
                q, n = step % 2, later_parts(step)
                lo, hi = n[0], n[-1] + 1
                g.tensor_tensor(rstd[:, q, lo:hi, :], ve[:, q, lo:hi, :], mhalf[:, lo:hi, :], ALU.pow).then_inc(s["roots"], 1)

            def mask(b, n):
                G = 4 * b + n
                pool.wait_ge(s["probs_ready"], G + 1)
                a = probs[:, G % PR, :, 0:2 * P]
                g.affine_select(out=a, in_=a, compare_op=ALU.is_ge, fill=0.0, base=0,
                                pattern=[[0, 2], [0, 2], [1, P]], channel_multiplier=-1).then_inc(s["masked"], 1)

            def gated(b):
                pool.wait_ge(s["xa_ready"], b + 1)
                if b:
                    pool.wait_ge(s["y_ps"], b)
                g.tensor_tensor(z[:, :], xa[:, :], gate[:, b % GR, :], ALU.mult).then_inc(s["z_ready"], 1)

            def scatter(n):
                c, k = n // TOPK, n % TOPK
                pool.wait_ge(s["rows_ready"], c + 1)
                if n == 0:
                    pool.wait_ge(s["slots_ready"], 1)
                    pool.wait_ge(s["slots_cleared"], 16)
                    pool.wait_ge(s["numbers_beside_rows"], 2)
                g.indirect_dma_start(slots_dram, bass.IndirectOffsetOnAxis(ap=slot[:, n:n + 1].bitcast(mybir.dt.uint32), axis=0),
                                     xrow[:, c, k, :], None).then_inc(s["scattered"], 16)

            pool.wait_ge(s["constants_ready"], 1)
            for b in range(AHEAD):
                root_x(b)
            mask(0, 0)
            sent = 0

            def scatters(b, place):
                nonlocal sent
                for _ in range(QUOTAS.get(b, (0, 0, 0))[place]):
                    scatter(sent)
                    sent += 1

            for b in range(B + 1):
                for n in (1, 2):
                    if b < B and by_pool(b, n):
                        mask(b, n)
                scatters(b, 0)
                if b + AHEAD < B:
                    root_x(b + AHEAD)
                if 2 <= b < LATE + 2:
                    gated(b - 2)
                if b >= 1:
                    root(b)
                scatters(b, 1)
                if b < B and by_pool(b, 3):
                    mask(b, 3)
                if b + 1 < B and by_pool(b + 1, 0):
                    mask(b + 1, 0)
                scatters(b, 2)
            assert sent == MC * TOPK

            def scatter_y(i, q):
                pool.wait_ge(s["yw_ready"], i + 1)
                number = xb[:, i, D:D + 1]
                g.indirect_dma_start(y_dram, bass.IndirectOffsetOnAxis(ap=number.bitcast(mybir.dt.uint32), axis=0),
                                     yw[q][:, :], None, bounds_check=NA - 1, oob_is_err=False).then_inc(y_out[q], 16)

            for i in range(NB):
                scatter_y(i, i % RING)

        @block.scalar
        def _(act):
            a = nc.scalar
            a.preload_act_table(ACT.Silu)
            act.wait_ge(s["bias_rows_in"], 48)
            a.activation(rows6_rh[:, :].rearrange("a (r h) -> a r h", h=H), rows6[:, :].rearrange("a (h r) -> a r h", r=HD), ACT.Copy).then_inc(s["rows_reordered"], 1)
            act.wait_ge(s["tables_ps"], 1)
            act.wait_ge(s["tables_zeroed"], 1)
            for r in range(3):
                a.activation(tabT[:, 0, 32 * r:32 * r + NEST], XB[:, 0:NEST], ACT.Copy)
                a.activation(tabT[:, 1, 32 * r + 16:32 * r + 16 + SEG], XB[:, 16:16 + SEG], ACT.Copy)
            a.activation(cols6[:, :, :], XB[:, 24:36].rearrange("p (o n) -> p o n", o=2), ACT.Copy)
            a.activation(posT[:, :, :], XB[:, 256:512].rearrange("p (c n) -> p c n", c=CH), ACT.Copy).then_inc(s["tabs_ready"], 1)
            act.wait_ge(s["products_ps"], 1)
            a.activation(raw[:, 0, :], XB[:, 256:256 + D], ACT.Copy).then_inc(s["raw_ready"], 1)
            a.activation(PW[:, :, :], XB[:, 0:256].rearrange("p (c n) -> p c n", c=CH), ACT.Copy).then_inc(s["positions_ready"], 1)
            act.wait_ge(s["weights_ps"], 1)
            for k in (0, 3):
                a.activation(W1T[:, k, :], PROJ[:, P * k:P * k + P], ACT.Copy).then_inc(s["weights_ready"], 1)
            a.activation(W1T[:, 1:3, :].rearrange("p k (r h) -> p k r h", h=H),
                         PROJ[:, P:3 * P].rearrange("p (k h r) -> p k r h", k=2, h=H), ACT.Copy).then_inc(s["weights_ready"], 1)
            a.activation(W2T[:, :], OUTC[:, 0:D], ACT.Copy).then_inc(s["weights_ready"], 1)
            act.wait_ge(s["tabs_ready"], 1)
            act.wait_ge(s["values_zeroed"], 1)

            def evac_x(b):
                act.wait_ge(s["xt_ps"], b + 1)
                if b >= 2:
                    act.wait_ge(s["gv_ps"], b - 1)
                a.activation(xT[:, b % 2, :], x_bank(b)[:, S:2 * S], ACT.Copy).then_inc(s["xt_ready"], 1)

            def project(b):
                q = b % 2
                act.wait_ge(s["qk_ps"], b + 1)
                if b >= 2:
                    act.wait_ge(s["third_pieces"], b - 1)
                for side in range(2):
                    a.activation(qk[:, q, side, :], PROJ[:, side * S:side * S + S], ACT.Silu,
                                 bias=(q_col, k_col)[side]).then_inc(s["qk_ready"], 1)

            def gate_v(b):
                q = b % R
                act.wait_ge(s["gv_ps"], b + 1)
                if b >= R:
                    act.wait_ge(s["av_done"], 2 * (b - R + 1))
                if b >= GR:
                    act.wait_ge(s["z_ready"], b - GR + 1)
                a.activation(gate[:, b % GR, :], gv_bank(b)[:, 0:S], ACT.Silu, bias=gate_col).then_inc(s["g_ready"], 1)
                src = gv_bank(b)[:, S:2 * S].rearrange("p (c j e r) -> p c j e r", c=CH, e=2, r=HD)
                for e in range(2):
                    a.activation(vpad[:, q, :, e::2, HD * e:HD * e + HD], src[:, :, :, e, :], ACT.Silu).then_inc(s["v_ready"], 1)

            def silu(b, n):
                G = 4 * b + n
                act.wait_ge(s["scores_ps"], G + 1)
                if G >= PR:
                    act.wait_ge(s["av_done"], (G - PR) // 2 + 1)
                i = 2 * (G % 2)
                for k in range(2):
                    last = a.activation(probs[:, G % PR, k, :], bank[SCORE[i + k]][:, 0:SC], ACT.Silu, scale=HD ** -0.5)
                last.then_inc(s["probs_ready"], 1)

            def evac_o(b):
                act.wait_ge(s["av_done"], 2 * b + 2)
                if b:
                    act.wait_ge(s["o_ps"], b)
                a.activation(oT[:, :], OTB[:, 0:S], ACT.Copy).then_inc(s["ot_ready"], 1)

            def affine(b):
                act.wait_ge(s["xot_ps"], b + 1)
                if b:
                    act.wait_ge(s["z_ready"], b)
                a.activation(xa[:, :], o_bank(b)[:, S:2 * S], ACT.Identity, scale=g_col, bias=b_col).then_inc(s["xa_ready"], 1)

            evac_x(0)
            project(0)
            evac_x(1)
            gate_v(0)
            project(1)
            evac_x(2)
            gate_v(1)
            project(2)
            gate_v(2)
            silu(0, 0)
            for b in range(B + 1):
                if b < B:
                    silu(b, 1)
                if b + 3 < B:
                    evac_x(b + 3)
                if 1 <= b <= B:
                    evac_o(b - 1)
                if b < B:
                    silu(b, 2)
                if b >= 2:
                    affine(b - 2)
                if b + 3 < B:
                    project(b + 3)
                if b < B:
                    silu(b, 3)
                if b + 1 < B:
                    silu(b + 1, 0)
                if b + 3 < B:
                    gate_v(b + 3)

            def gelu(i, q, first):
                act.wait_ge(s["hid_ps"], i + 1)
                if not first:
                    act.wait_ge(s["ye_ps"], i - RING + 1)
                a.activation(hid[q][:, :], bank[q][:, :], ACT.Gelu).then_inc(s["hid_ready"], 1)

            gelu(0, 0, True)
            affine(B - 1)
            for i in range(1, RING):
                gelu(i, i, True)
            with act.Fori(RING, LOOPED, RING) as i:
                for q in range(RING):
                    gelu(i + q, q, False)
            for i in range(LOOPED, NB):
                gelu(i, i % RING, False)

        @block.vector
        def _(dve):
            v = nc.vector
            v.memset(ones_bf[:, :], 1.0).then_inc(s["ones_ready"], 1)
            v.memset(mhalf[:, :, :], -0.5).then_inc(s["constants_ready"], 1)
            v.memset(tabT[:, :, :], 0.0).then_inc(s["tables_zeroed"], 1)
            v.memset(raw[:, 1:3, :], 0.0).then_inc(s["raw_zeroed"], 1)
            v.memset(zeros8[:, :], 0.0)
            v.memset(zeroB[:, :], 0.0).then_inc(s["constants_ready"], 1)
            dve.wait_ge(s["ids_in"], 16)
            opens, closes = (40, 91, 123), (41, 93, 125)
            v.tensor_scalar(cmpf[:, 6, :], ids[:, :], 39990.0, None, ALU.is_gt).then_inc(s["segment_marks"], 1)
            for n in range(3):
                for sign, codes, done in ((0, opens, "opens_found"), (3, closes, "closes_found")):
                    if n == 0:
                        v.tensor_scalar(cmpf[:, sign, :], ids[:, :], float(codes[0]), None, ALU.is_equal).then_inc(s[done], 1)
                    else:
                        dve.wait_ge(s[done], n)
                        v.scalar_tensor_tensor(cmpf[:, sign + n, :], ids[:, :], float(codes[n]), cmpf[:, sign + n - 1, :],
                                               ALU.is_equal, ALU.add).then_inc(s[done], 1)
                if n == 0:
                    dve.wait_ge(s["constants_ready"], 2)
                    dve.wait_ge(s["segment_marks"], 1)
                    v.tensor_tensor_scan(segf[:, :], cmpf[:, 6, :], zeroB[:, :], 0.0, ALU.add, ALU.add).then_inc(s["segments_ready"], 1)
            dve.wait_ge(s["opens_found"], 3)
            dve.wait_ge(s["closes_found"], 3)
            v.tensor_tensor(delta[:, :], cmpf[:, 2, :], cmpf[:, 5, :], ALU.subtract).then_inc(s["steps_ready"], 1)
            dve.wait_ge(s["segments_ready"], 1)
            v.tensor_copy(segi[:, :], segf[:, :]).then_inc(s["segments_ready"], 1)
            dve.wait_ge(s["steps_ready"], 1)
            v.tensor_tensor_scan(depth[:, :], delta[:, :], zeroB[:, :], 0.0, ALU.add, ALU.add).then_inc(s["depth_ready"], 1)
            dve.wait_ge(s["segments_ready"], 2)
            v.tensor_scalar(segi8[:, :], segi[:, :], 7, None, ALU.bitwise_and).then_inc(s["segments_ready"], 1)
            dve.wait_ge(s["depth_ready"], 1)
            v.tensor_tensor_scan(lowest[:, :], depth[:, :], zeroB[:, :], 0.0, ALU.min, ALU.min).then_inc(s["lowest_ready"], 1)
            dve.wait_ge(s["lowest_ready"], 1)
            v.tensor_tensor(nestf[:, :], depth[:, :], lowest[:, :], ALU.subtract).then_inc(s["nest_ready"], 1)
            dve.wait_ge(s["nest_ready"], 1)
            v.tensor_scalar(code[:, 0, :], nestf[:, :], 0.0, float(NEST - 1), ALU.max, ALU.min).then_inc(s["code_ready"], 1)
            dve.wait_ge(s["segments_ready"], 3)
            v.tensor_copy(code[:, 1, :], segi8[:, :]).then_inc(s["code_ready"], 1)
            dve.wait_ge(s["numbers_ready"], 1)
            v.tensor_scalar(row32[:, :], rowi[:, :], 31, None, ALU.bitwise_and).then_inc(s["row_codes"], 1)
            dve.wait_ge(s["row_codes"], 1)
            v.tensor_copy(rowf[:, :], row32[:, :]).then_inc(s["row_codes"], 1)
            dve.wait_ge(s["row_codes"], 2)
            v.tensor_scalar(rowge[:, :], rowf[:, :], 16.0, -16.0, ALU.is_ge, ALU.mult).then_inc(s["row_codes"], 1)
            dve.wait_ge(s["row_codes"], 3)
            v.tensor_tensor(rowcode[:, :], rowf[:, :], rowge[:, :], ALU.add).then_inc(s["row_codes"], 1)
            dve.wait_ge(s["row_codes"], 4)

            def spread(n):
                dve.wait_ge(s["code_ps"], n + 1)
                v.tensor_scalar(onehot[:, 2 * n:2 * n + 2, :], bank[SCORE[n]][:, :].rearrange("p (b s) -> p b s", b=2),
                                rowcode[:, 0:1], None, ALU.is_equal).then_inc(s["onehot_ready"], 1)

            dve.wait_ge(s["raw_ready"], 1)
            dve.wait_ge(s["bias_pieces_in"], 96)
            v.tensor_copy(rhs_pieces[:, :, :], raw[:, :, :]).then_inc(s["first_piece_ready"], 1)
            dve.wait_ge(s["first_piece_ready"], 1)
            v.tensor_tensor(rest[:, :, :], raw[:, :, :], rhs_pieces[:, :, :], ALU.subtract).then_inc(s["rest_ready"], 1)
            spread(0)
            dve.wait_ge(s["rest_ready"], 1)
            v.tensor_copy(rhs_pieces[32:64, :, :], rest[32:64, :, :])
            v.tensor_copy(piece2[64:96, :, :], rest[64:96, :, :]).then_inc(s["second_piece_ready"], 1)
            v.memset(rhs_pieces[96:128, :, :], 0.0)
            dve.wait_ge(s["second_piece_ready"], 1)
            v.tensor_tensor(rhs_pieces[64:96, :, :], rest[64:96, :, :], piece2[64:96, :, :], ALU.subtract).then_inc(s["pieces_ready"], 1)
            spread(1)
            dve.wait_ge(s["positions_ready"], 1)

            def embed(b):
                q = b % 2
                hb = h_all[:, CH * b:CH * b + CH, :]
                dve.wait_ge(s["embed_ps"], b + 1)
                v.tensor_tensor(hb, x_bank(b)[:, 0:S].rearrange("p (c n) -> p c n", c=CH), PW[:, :, :], ALU.add).then_inc(s["h_ready"], 1)

            def statistics_x(b):
                dve.wait_ge(s["h_ready"], b + 1)
                for c in range(CH):
                    v.bn_stats(bst[:, b % 2, STAT_X, c, :], h_all[:, CH * b + c, :]).then_inc(s["x_stats"], 1)
                for c in range(CH):
                    dve.wait_ge(s["x_stats"], CH * b + c + 1)
                    v.bn_aggr(mv[:, b % 2, STAT_X, c, :], bst[:, b % 2, STAT_X, c, :]).then_inc(s["x_moments"], 1)
                dve.wait_ge(s["x_moments"], CH * (b + 1))
                v.tensor_scalar(ve[:, b % 2, STAT_X, :], mv[:, b % 2, STAT_X, :, 1], EPS, None, ALU.add).then_inc(s["x_variances"], 1)

            made = 0

            def statistics(step):
                nonlocal made
                q, n = step % 2, later_parts(step)
                if STAT_H in n:
                    dve.wait_ge(s["h2_ready"], step - 2)
                for part in reversed(n):
                    if part == STAT_O:
                        dve.wait_ge(s["o_ps"], step)
                    for c in range(CH):
                        src = o_bank(step - 1)[:, P * c:P * c + P] if part == STAT_O else h_all[:, CH * (step - 3) + c, :]
                        v.bn_stats(bst[:, q, part, c, :], src).then_inc(s["stats"], 1)
                for part in reversed(n):
                    for c in range(CH):
                        made += 1
                        dve.wait_ge(s["stats"], made)
                        v.bn_aggr(mv[:, q, part, c, :], bst[:, q, part, c, :]).then_inc(s["moments"], 1)
                dve.wait_ge(s["moments"], made)
                v.tensor_scalar(ve[:, q, n[0]:n[-1] + 1, :], mv[:, q, n[0]:n[-1] + 1, :, 1], EPS, None, ALU.add).then_inc(s["variances"], 1)

            def normalise(b):
                q = p = b % 2
                dve.wait_ge(s["x_roots"], b + 1)
                if b >= 2:
                    dve.wait_ge(s["xt_ps"], b - 1)
                for c in range(CH):
                    v.tensor_scalar(xn[:, q, c, :], h_all[:, CH * b + c, :], mv[:, p, STAT_X, c, 0:1], rstd[:, p, STAT_X, c:c + 1],
                                    ALU.subtract, ALU.mult).then_inc(s["xn_ready"], 1)

            def split_first(b):
                q = b % 2
                dve.wait_ge(s["qk_ready"], 2 * (b + 1))
                if b >= 2:
                    dve.wait_ge(stk[(b - 2) % R], 16 * len(PIECES) * ((b - 2) // R + 1))
                v.tensor_copy(qkp[:, q, :, 0, :], qk[:, q, :, :]).then_inc(s["first_pieces"], 1)

            def split_rest(b):
                q = b % 2
                dve.wait_ge(s["first_pieces"], b + 1)
                v.tensor_tensor(qkr[:, q, :, :], qk[:, q, :, :], qkp[:, q, :, 0, :], ALU.subtract).then_inc(s["remainders"], 1)
                if b >= AHEAD:
                    normalise2(b - AHEAD, 0)
                dve.wait_ge(s["remainders"], b + 1)
                v.tensor_copy(qkp[:, q, :, 1, :], qkr[:, q, :, :]).then_inc(s["second_pieces"], 1)
                if b >= AHEAD:
                    normalise2(b - AHEAD, 1)
                dve.wait_ge(s["second_pieces"], b + 1)
                v.tensor_tensor(qkp[:, q, :, 2, :], qkr[:, q, :, :], qkp[:, q, :, 1, :], ALU.subtract).then_inc(s["third_pieces"], 1)

            def normalise2(b, c):
                p = (b + 1) % 2
                dve.wait_ge(s["roots"], b + 1)
                if b:
                    dve.wait_ge(s["xot_ps"], b)
                v.tensor_scalar(xo[:, c, :], o_bank(b)[:, P * c:P * c + P], mv[:, p, STAT_O, c, 0:1], rstd[:, p, STAT_O, c:c + 1],
                                ALU.subtract, ALU.mult).then_inc(s["xo_ready"], 1)

            def mask(b, n):
                G = 4 * b + n
                if masked_before(b, n)[1] == 1:
                    dve.wait_ge(s["future_ready"], 2)
                dve.wait_ge(s["probs_ready"], G + 1)
                last = v.copy_predicated(probs[:, G % PR, :, 0:2 * P].rearrange("p a (t n) -> p a t n", n=P),
                                         future[:, :].unsqueeze(1).unsqueeze(1).to_broadcast([P, 2, 2, P]),
                                         zeros[:, :].unsqueeze(1).unsqueeze(1).to_broadcast([P, 2, 2, P]))
                last.then_inc(s["masked_dve"], 1)

            def gated(b):
                dve.wait_ge(s["xa_ready"], b + 1)
                dve.wait_ge(s["y_ps"], b)
                v.tensor_tensor(z[:, :], xa[:, :], gate[:, b % GR, :], ALU.mult).then_inc(s["z_ready"], 1)

            def residual(b):
                hb = h_all[:, CH * b:CH * b + CH, :]
                dve.wait_ge(s["y_ps"], b + 1)
                v.tensor_tensor(hb, XB[:, S:2 * S].rearrange("p (c n) -> p c n", c=CH), hb, ALU.add).then_inc(s["h2_ready"], 1)

            def normalise3(b):
                p = (b + 3) % 2
                dve.wait_ge(s["roots"], b + 3)
                for c in range(CH):
                    n = CH * b + c
                    v.tensor_scalar(xrow[:, n, :, 0:D], h_all[:, n, :].unsqueeze(1).to_broadcast([P, TOPK, D]),
                                    mv[:, p, STAT_H, c, 0:1], rstd[:, p, STAT_H, c:c + 1], ALU.subtract, ALU.mult).then_inc(s["rows_ready"], 1)

            NJ = MC * TOPK

            def count_routes():
                dve.wait_ge(s["routes_in"], 32)
                v.tensor_copy(re_f[:, :], re_i[:, :, :].rearrange("p c k -> p (c k)")).then_inc(s["experts_read"], 1)
                v.memset(restart[:, :, :], 1.0).then_inc(s["restarts_ready"], 1)
                dve.wait_ge(s["experts_read"], 1)
                for e in range(E):
                    last = v.tensor_scalar(chosen[:, e, :], re_f[:, :], float(e), None, ALU.is_equal)
                last.then_inc(s["choices_ready"], 1)
                dve.wait_ge(s["restarts_ready"], 1)
                v.memset(restart[:, :, 0:1], 0.0).then_inc(s["restarts_ready"], 1)
                dve.wait_ge(s["restarts_ready"], 2)
                dve.wait_ge(s["choices_ready"], 1)
                v.tensor_tensor_scan(rank[:, :, :].rearrange("p e j -> p (e j)"), restart[:, :, :].rearrange("p e j -> p (e j)"),
                                     chosen[:, :, :].rearrange("p e j -> p (e j)"), 0.0, ALU.mult, ALU.add).then_inc(s["ranked"], 1)
                dve.wait_ge(s["ranked"], 1)
                v.tensor_copy(count_bf[:, :], rank[:, :, NJ - 1]).then_inc(s["counted"], 1)

            steps = 0

            def then(ins):
                nonlocal steps
                steps += 1
                ins.then_inc(s["routing_steps"], 1)
                dve.wait_ge(s["routing_steps"], steps)

            def expert_blocks():
                dve.wait_ge(s["prefix_ps"], 1)
                v.tensor_copy(prefix[:, :, :], OUTC[:, 0:2 * E].rearrange("p (a e) -> p a e", a=2)).then_inc(s["prefix_ready"], 1)
                dve.wait_ge(s["prefix_ready"], 1)
                then(v.tensor_scalar(full_i[:, :], prefix[:, 1, :], float(P - 1), None, ALU.add))
                then(v.tensor_scalar(blocks_i[:, :], full_i[:, :], P.bit_length() - 1, None, ALU.arith_shift_right))
                then(v.tensor_copy(blocks[:, :], blocks_i[:, :]))
                then(v.tensor_tensor_scan(ends[:, :], blocks[:, :], zeros8[:, :], 0.0, ALU.add, ALU.add))
                then(v.tensor_tensor(starts[:, :], ends[:, :], blocks[:, :], ALU.subtract))
                then(v.scalar_tensor_tensor(offset[:, :], starts[:, :], float(P), prefix[:, 0, :], ALU.mult, ALU.add))

            def assignment_slots():
                then(v.tensor_tensor(place[:, :, :], rank[:, :, :], offset[:, :].unsqueeze(2).to_broadcast([P, E, NJ]), ALU.add))
                then(v.tensor_tensor(placed[:, :, :], place[:, :, :], chosen[:, :, :], ALU.mult))
                then(v.tensor_reduce(slot_f[:, :], placed[:, :, :].rearrange("p e j -> p j e"), mybir.AxisListType.X, ALU.add))
                v.tensor_scalar(slot[:, :], slot_f[:, :], -1.0, None, ALU.add).then_inc(s["slots_ready"], 1)

            def block_owners():
                dve.wait_ge(s["numbers_ready"], 2)
                then(v.tensor_tensor(passed[:, :, :], block_no[:, :, :], ends[:, :].unsqueeze(1).to_broadcast([P, NB, E]), ALU.is_ge))
                then(v.tensor_reduce(owner_f[:, :], passed[:, :, :], mybir.AxisListType.X, ALU.add))
                v.tensor_scalar(owner[:, :], owner_f[:, :], float(E - 1), None, ALU.min).then_inc(s["owner_ready"], 1)

            embed(0)
            statistics_x(0)
            embed(1)
            statistics_x(1)
            normalise(0)
            spread(2)
            embed(2)
            statistics_x(2)
            normalise(1)
            spread(3)
            embed(3)
            statistics_x(3)
            for b in range(AHEAD - 1):
                split_first(b)
                if b < 2:
                    normalise(b + 2)
                split_rest(b)
            count_routes()
            for b in range(B + 1):
                if b + 4 < B:
                    embed(b + 4)
                    statistics_x(b + 4)
                for n in (0, 1):
                    if b < B and not by_pool(b, n):
                        mask(b, n)
                if b >= LATE + 2:
                    gated(b - 2)
                if b >= 1:
                    statistics(b)
                for n in (2, 3):
                    if b < B and not by_pool(b, n):
                        mask(b, n)
                if b + 4 < B:
                    normalise(b + 4)
                if b + 3 < B:
                    split_first(b + 3)
                if b >= 2:
                    residual(b - 2)
                if b + 3 < B:
                    split_rest(b + 3)
                elif b <= B:
                    for c in range(CH):
                        normalise2(b - 1, c)
                if b == 0:
                    expert_blocks()
                if b == 1:
                    assignment_slots()
                if b == 2:
                    block_owners()
                    dve.wait_ge(s["below_ready"], 1)
                    v.tensor_scalar(future[:, :], below[:, :], 0.0, None, ALU.is_gt).then_inc(s["future_ready"], 1)
                    v.memset(zeros[:, :], 0.0).then_inc(s["future_ready"], 1)
                if 3 <= b < 3 + TM // S:
                    normalise3(b - 3)

            for j, (n, m) in enumerate(XB_PARTS):
                dve.wait_ge(s["xbt_ps"], j + 1)
                v.tensor_copy(xbT[:, P * n:P * (n + m)], bank[SLOT_BANKS[j]][:, 0:P * m]).then_inc(s["xbt_ready"], 1)
                if j == 1:
                    gated(B - 1)
                    residual(B - 1)

            def weigh(i, q, first):
                dve.wait_ge(s["ye_ps"], i + 1)
                if not first:
                    dve.wait_ge(y_out[q], (i - q) * (16 // RING))
                v.tensor_scalar(yw[q][:, :], bank[6 + q % 2][:, 0:D], xb[:, bass.ds(i, 1), D + 1], None, ALU.mult).then_inc(s["yw_ready"], 1)

            for i in range(RING):
                weigh(i, i, True)
            with dve.Fori(RING, LOOPED, RING) as i:
                for q in range(RING):
                    weigh(i + q, q, False)
            for i in range(LOOPED, NB):
                weigh(i, i % RING, False)
            for n in range(0, MC, 2):
                dve.wait_ge(yb_in[n // 2], 16)
                v.tensor_tensor(ysum[:, n:n + 2, :], yb[:, n:n + 2, 0, :], yb[:, n:n + 2, 1, :], ALU.add).then_inc(s["ysum_ready"], 1)
                if n:
                    dve.wait_ge(s["ysum_ready"], n // 2)
                    v.tensor_tensor(ysum[:, n - 2:n, :], ysum[:, n - 2:n, :], h_all[:, n - 2:n, :], ALU.add).then_inc(s["out_ready"], 1)
            dve.wait_ge(s["ysum_ready"], MC // 2)
            v.tensor_tensor(ysum[:, MC - 2:MC, :], ysum[:, MC - 2:MC, :], h_all[:, MC - 2:MC, :], ALU.add).then_inc(s["out_ready"], 1)

        @block.tensor
        def _(pe):
            mm = nc.tensor.matmul
            tr = nc.tensor.transpose

            pe.wait_ge(s["ones_ready"], 1)
            pe.wait_ge(s["ident_ready"], 1)
            pe.wait_ge(s["tables_in"], 48)
            tr(XB[:, 0:NEST], nest_sb[:, :], ident[0:NEST, 0:NEST])
            tr(XB[:, 16:16 + SEG], seg_sb[:, :], ident[0:SEG, 0:SEG])
            pe.wait_ge(s["bias_rows_in"], 48)
            tr(XB[:, 24:30], rows6[:, :], ident[0:6, 0:6])
            pe.wait_ge(s["rows_reordered"], 1)
            tr(XB[:, 30:36], rows6_rh[:, :], ident[0:6, 0:6])
            for c in range(CH):
                last = tr(XB[:, 256 + P * c:256 + P * c + P], pos_sb[:, c, :], ident[:, :])
            last.then_inc(s["tables_ps"], 1)
            def spread(n):
                for b in (2 * n, 2 * n + 1):
                    dst = bank[SCORE[n]][:, S * (b % 2):S * (b % 2) + S]
                    mm(dst, sel[:, 0, b, :], code[:, 0, :], start=True, stop=False)
                    last = mm(dst, sel[:, 1, b, :], code[:, 1, :], start=False, stop=True)
                last.then_inc(s["code_ps"], 1)

            pe.wait_ge(s["tabs_ready"], 1)
            pe.wait_ge(s["tokw_in"], 16)
            mm(XB[:, 256:256 + D], tabT[:, 0, :], tokW_sb[:, 1, :], start=True, stop=False)
            mm(XB[:, 256:256 + D], tabT[:, 1, :], tokW_sb[:, 2, :], start=False, stop=True)
            for c in range(CH):
                last = mm(XB[:, P * c:P * c + P], posT[:, c, :], tokW_sb[:, 0, :], start=True, stop=True)
            last.then_inc(s["products_ps"], 1)
            pe.wait_ge(s["code_ready"], 2)
            pe.wait_ge(s["sel_ready"], 2)
            for n in range(B // 2 - 1):
                spread(n)
            pe.wait_ge(s["attnw_in"], 32)
            for k in range(4):
                tr(PROJ[:, P * k:P * k + P], W1_sb[:, k, :], ident[:, :])
            tr(OUTC[:, 0:D], W2_sb[:, :], ident[:, :]).then_inc(s["weights_ps"], 1)

            def embed(b):
                pe.wait_ge(s["onehot_ready"], b // 2 + 1)
                if b == 0:
                    pe.wait_ge(s["pieces_ready"], 1)
                if b == 2:
                    pe.wait_ge(s["weights_ready"], 4)
                if b == AHEAD - 1:
                    pe.wait_ge(s["positions_ready"], 1)
                if b >= AHEAD:
                    pe.wait_ge(s["xt_ready"], b)
                    pe.wait_ge(s["h_ready"], b)
                for c in range(CH):
                    last = mm(x_bank(b)[:, P * c:P * c + P], onehot[:, b, P * c:P * c + P], rhs_pieces[:, 0, :], start=True, stop=True)
                last.then_inc(s["embed_ps"], 1)

            def transpose_x(b):
                pe.wait_ge(s["xn_ready"], CH * (b + 1))
                if b >= AHEAD + 2:
                    pe.wait_ge(s["h2_ready"], b - AHEAD - 1)
                pe.wait_ge(s["h_ready"], b + 1)
                for c in range(CH):
                    last = tr(x_bank(b)[:, S + P * c:S + P * c + P], xn[:, b % 2, c, :], ident[:, :])
                last.then_inc(s["xt_ps"], 1)

            def project_qk(b):
                pe.wait_ge(s["xt_ready"], b + 1)
                if b == 0:
                    pe.wait_ge(s["weights_ready"], 4)
                elif b < AHEAD:
                    pe.wait_ge(s["qk_ready"], 2 * b)
                else:
                    pe.wait_ge(s["v_ready"], 2 * b)
                for side in range(2):
                    last = mm(PROJ[:, side * S:side * S + S], W1T[:, 1 + side, :], xT[:, b % 2, :], start=True, stop=True)
                last.then_inc(s["qk_ps"], 1)

            def project_gv(b):
                dst = gv_bank(b)
                if b < AHEAD - 1:
                    pe.wait_ge(s["onehot_ready"], b + 2)
                else:
                    pe.wait_ge(s["qk_ready"], 2 * (b + 1))
                mm(dst[:, 0:S], W1T[:, 0, :], xT[:, b % 2, :], start=True, stop=True)
                for c in range(CH):
                    v_part = dst[:, S + P * c:S + P * c + P]
                    mm(v_part, xT[:, b % 2, P * c:P * c + P], W1T[:, 3, :], start=True, stop=False)
                    last = mm(v_part, ones_bf[:, :], rhs_pieces[:, 1, :], start=False, stop=True)
                last.then_inc(s["gv_ps"], 1)

            def scores(b, n):
                G, q = 4 * b + n, b % R
                if n == 0:
                    pe.wait_ge(stk[q], 16 * len(PIECES) * (b // R + 1))
                if G >= 2:
                    pe.wait_ge(s["probs_ready"], G - 1)
                else:
                    pe.wait_ge(s["v_ready"], (2, 2 * (AHEAD - 1))[G])
                i = 2 * (G % 2)
                for k, h in enumerate(HALVES[n // 2][2 * (n % 2):2 * (n % 2) + 2]):
                    dst, kk, qq = bank[SCORE[i + k]], stacks[:, q, h, 1, :], stacks[:, q, h, 0, :]
                    mm(dst[:, P:SC], kk[:, 0:P], qq, start=True, stop=True)
                    last = mm(dst[:, 0:P], kk[:, P:S], qq[:, P:S], start=True, stop=True)
                last.then_inc(s["scores_ps"], 1)

            def attend(b, half):
                q = b % R
                by_gpsimd, by_vector = masked_before(b, 2 * half + 1)
                pe.wait_ge(s["masked"], by_gpsimd)
                if by_vector:
                    pe.wait_ge(s["masked_dve"], by_vector)
                if half == 0:
                    pe.wait_ge(s["v_ready"], 2 * (b + 1))
                    if b:
                        pe.wait_ge(s["ot_ready"], b)
                for c in range(CH):
                    for j, h in enumerate(HALVES[half]):
                        pr = probs[:, (4 * b + 2 * half + j // 2) % PR, j % 2, :]
                        dst = OTB[32 * j:32 * j + 32, P * c:S]
                        last = mm(dst, vpad[:, q, c, h, :], pr[:, P:SC] if c == 0 else pr[:, 0:P],
                                  start=(half == 0 and c == 0), stop=(half == 1 and c == 1), skip_group_check=True)
                last.then_inc(s["av_done"], 1)

            def transpose_o(b):
                pe.wait_ge(s["ot_ready"], b + 1)
                if b == 0:
                    pe.wait_ge(s["prefix_ready"], 1)
                elif b < AHEAD:
                    pe.wait_ge(s["xa_ready"], b)
                elif b == AHEAD:
                    pe.wait_ge(s["v_ready"], 2 * B)
                else:
                    pe.wait_ge(s["xa_ready"], b - 1)
                for c in range(CH):
                    last = tr(o_bank(b)[:, P * c:P * c + P], oT[:, P * c:P * c + P], ident[:, :])
                last.then_inc(s["o_ps"], 1)

            def transpose_xo(b):
                pe.wait_ge(s["xo_ready"], CH * (b + 1))
                for c in range(CH):
                    last = tr(o_bank(b)[:, S + P * c:S + P * c + P], xo[:, c, :], ident[:, :])
                last.then_inc(s["xot_ps"], 1)

            def out_proj(b):
                pe.wait_ge(s["z_ready"], b + 1)
                pe.wait_ge(s["h_ready"], min(b + 3 + AHEAD, B))
                if b:
                    pe.wait_ge(s["h2_ready"], b)
                for c in range(CH):
                    dst = XB[:, S + P * c:S + P * c + P]
                    mm(dst, z[:, P * c:P * c + P], W2T[:, :], start=True, stop=False)
                    last = mm(dst, ones_bf[:, :], rhs_pieces[:, 2, :], start=False, stop=True)
                last.then_inc(s["y_ps"], 1)

            embed(0)
            embed(1)
            spread(B // 2 - 1)
            embed(2)
            embed(3)
            transpose_x(0)
            project_qk(0)
            transpose_x(1)
            project_gv(0)
            project_qk(1)
            transpose_x(2)
            project_gv(1)
            project_qk(2)
            project_gv(2)
            scores(0, 0)
            for b in range(B + 1):
                if b < B:
                    scores(b, 1)
                if b >= 1:
                    attend(b - 1, 1)
                if b + 3 < B:
                    transpose_x(b + 3)
                if b < B:
                    scores(b, 2)
                if b + 4 < B:
                    embed(b + 4)
                if b >= 2:
                    transpose_xo(b - 2)
                if b + 3 < B:
                    project_qk(b + 3)
                if b < B:
                    scores(b, 3)
                if b >= 1:
                    transpose_o(b - 1)
                if b + 1 < B:
                    scores(b + 1, 0)
                if b + 3 < B:
                    project_gv(b + 3)
                if b >= 2:
                    out_proj(b - 2)
                if b == 0:
                    pe.wait_ge(s["upper_ready"], 1)
                    pe.wait_ge(s["counted"], 1)
                    mm(OUTC[:, 0:E], upper[:, :], count_bf[:, :], start=True, stop=True)
                    mm(OUTC[:, E:2 * E], ones_bf[:, :], count_bf[:, :], start=True, stop=True).then_inc(s["prefix_ps"], 1)
                if b < B:
                    attend(b, 0)

            def transpose_slots(j):
                n, m = XB_PARTS[j]
                pe.wait_ge(xb_in[j], 16)
                if j == 0:
                    pe.wait_ge(s["xa_ready"], B - 1)
                elif j in (1, 3):
                    pe.wait_ge(s["probs_ready"], 4 * B)
                elif j == 5:
                    pe.wait_ge(s["xa_ready"], B)
                elif j:
                    pe.wait_ge(s["xbt_ready"], j - 1)
                for i in range(m):
                    last = tr(bank[SLOT_BANKS[j]][:, P * i:P * i + P], xb[:, n + i, 0:D], ident[:, :])
                last.then_inc(s["xbt_ps"], 1)

            def up(i, q, first):
                pe.wait_ge(w1_in[q], 16 * (i // RING + 1) if isinstance(i, int) else (i + RING - q) * (16 // RING))
                if not first:
                    pe.wait_ge(s["hid_ready"], i - RING + 1)
                for f in range(FC):
                    last = mm(bank[q][:, P * f:P * f + P], w1s[q][:, P * f:P * f + P], xbT[:, bass.ds(i * P, P)], start=True, stop=True)
                last.then_inc(s["hid_ps"], 1)

            def down(i, q, first):
                pe.wait_ge(s["hid_ready"], i + 1)
                if not first:
                    pe.wait_ge(s["yw_ready"], i - 1)
                e = pe.value_load(owner[0:1, bass.ds(i, 1)], min_val=0, max_val=E - 1)
                for f in range(FC):
                    last = mm(bank[6 + q % 2][:, 0:D], hid[q][:, P * f:P * f + P], w2_sb[:, bass.ds(e * (FC * D) + f * D, D)],
                              start=(f == 0), stop=(f == FC - 1))
                last.then_inc(s["ye_ps"], 1)

            pe.wait_ge(s["probs_ready"], 4 * B)
            for _ in range(64):
                mm(bank[0][:, 0:P], ones_bf[:, :], ones_bf[:, :], start=True, stop=True)
            transpose_slots(0)
            transpose_slots(1)
            pe.wait_ge(s["xbt_ready"], 1)
            up(0, 0, True)
            transpose_xo(B - 1)
            transpose_slots(2)
            up(1, 1, True)
            transpose_slots(3)
            out_proj(B - 1)
            pe.wait_ge(s["xbt_ready"], 2)
            up(2, 2, True)
            pe.wait_ge(s["owner_ready"], 1)
            pe.wait_ge(s["w2_in"], 16 * (B // 2))
            down(0, 0, True)
            transpose_slots(4)
            transpose_slots(5)
            pe.wait_ge(s["xbt_ready"], 4)
            up(3, 3, True)
            pe.wait_ge(s["h2_ready"], B)
            down(1, 1, True)
            pe.wait_ge(s["xbt_ready"], len(XB_PARTS))
            with pe.Fori(RING, LOOPED, RING) as i:
                for q in range(RING):
                    up(i + q, q, False)
                    down(i + q - 2, (q - 2) % RING, False)
            for i in range(LOOPED, NB):
                up(i, i % RING, False)
                down(i - 2, (i - 2) % RING, False)
            for i in range(NB - 2, NB):
                down(i, i % RING, False)


_INS = ["x", "L0_tok_pos_table", "L0_tok_nest_table", "L0_tok_seg_table", "L0_tok_W", "L0_attn_W1", "L0_attn_b1",
        "L0_attn_ln_g", "L0_attn_ln_b", "L0_attn_W2", "L0_attn_b2", "L0_ffn_expert_weights", "L0_ffn_expert_indices",
        "L0_ffn_w1", "L0_ffn_w2"]


def kernel(**inputs):
    import numpy as np
    import concourse.bacc as bacc
    from concourse import mybir
    from concourse.bass_utils import run_bass_kernel_spmd

    nc = bacc.Bacc("TRN2", target_bir_lowering=False, num_devices=1)
    arrays, args = {}, []
    for name in _INS:
        a = np.ascontiguousarray(inputs[name])
        arrays[f"in_{name}"] = a
        args.append(nc.dram_tensor(f"in_{name}", a.shape, mybir.dt.from_np(a.dtype), kind="ExternalInput").ap())
    out = nc.dram_tensor("out", (8, 256, 128), mybir.dt.float32, kind="ExternalOutput").ap()
    build(nc, *args, out)
    r = run_bass_kernel_spmd(nc, [arrays], core_ids=[0])
    return r.results[0]["out"]
```
